# Optimizing a Trainium2 kernel written in Bass

```python
import numpy as np
import jax
import jax.numpy as jnp

def _softmax(x, axis=-1):
    return jax.nn.softmax(x, axis=axis)

def _gelu(x):
    return jax.nn.gelu(x, approximate=True)

def _silu(x):
    return jax.nn.silu(x)

def _sigmoid(x):
    return jax.nn.sigmoid(x)

def _layernorm(x, axis=-1, eps=1e-05):
    m = jnp.mean(x, axis=axis, keepdims=True)
    v = jnp.var(x, axis=axis, keepdims=True)
    return (x - m) / jnp.sqrt(v + eps)

def _scatter_add(tgt, idx, src, axis=0):
    return tgt.at[idx].add(src)

def _segment_sum(src, seg, n):
    return jax.ops.segment_sum(src, seg, n)
kernel_name = 'mk_prb_d1_jaxref_r4_f4e4ec'

def setup_inputs(seed: int=0):
    np.random.seed(seed)
    _w = jnp.asarray

    def _L0_attn_setup():
        import jax, jax.numpy as jnp
        import numpy as np
        B, L, E, H = (2, 256, 256, 16)
        D = E // H
        EPS = 1e-06

        def rmsnorm(x, w, eps=1e-06):
            var = jnp.mean(jnp.square(x), axis=-1, keepdims=True)
            return x * jax.lax.rsqrt(var + eps) * w

        def cosformer_attn(x, qkv_w, qkv_b, out_w, out_b):
            b, l, e = x.shape
            qkv = x @ qkv_w + qkv_b
            q, k, v = jnp.split(qkv, 3, axis=-1)
            q = q.reshape(b, l, H, D).transpose(0, 2, 1, 3)
            k = k.reshape(b, l, H, D).transpose(0, 2, 1, 3)
            v = v.reshape(b, l, H, D).transpose(0, 2, 1, 3)
            positions = jnp.arange(l, dtype=jnp.float32).reshape(1, 1, l, 1)
            cos_w = jnp.cos(jnp.pi / 2 * positions / l)
            sin_w = jnp.sin(jnp.pi / 2 * positions / l)
            q_prime = jax.nn.relu(q)
            k_prime = jax.nn.relu(k)
            q_cos, q_sin = (q_prime * cos_w, q_prime * sin_w)
            k_cos, k_sin = (k_prime * cos_w, k_prime * sin_w)
            kv_cos_cumsum = jnp.cumsum(jnp.einsum('bhld,bhle->bhlde', k_cos, v), axis=2)
            context_cos = jnp.einsum('bhld,bhlde->bhle', q_cos, kv_cos_cumsum)
            kv_sin_cumsum = jnp.cumsum(jnp.einsum('bhld,bhle->bhlde', k_sin, v), axis=2)
            context_sin = jnp.einsum('bhld,bhlde->bhle', q_sin, kv_sin_cumsum)
            context = context_cos + context_sin
            k_cos_cumsum = jnp.cumsum(k_cos, axis=2)
            k_sin_cumsum = jnp.cumsum(k_sin, axis=2)
            norm = jnp.einsum('bhld,bhld->bhl', q_cos, k_cos_cumsum) + jnp.einsum('bhld,bhld->bhl', q_sin, k_sin_cumsum)
            output = context / (norm[..., None] + EPS)
            output = output.transpose(0, 2, 1, 3).reshape(b, l, e)
            return output @ out_w + out_b
        key = jax.random.key(seed)
        ks = jax.random.split(key, 6)
        x = jax.random.normal(ks[0], (B, L, E), dtype=jnp.float32)
        qkv_w = jax.random.normal(ks[1], (E, 3 * E), dtype=jnp.float32) / np.sqrt(E)
        qkv_b = jnp.zeros((3 * E,), dtype=jnp.float32)
        out_w = jax.random.normal(ks[2], (E, E), dtype=jnp.float32) / np.sqrt(E)
        out_b = jnp.zeros((E,), dtype=jnp.float32)
        norm1_w = jnp.ones((E,), dtype=jnp.float32)
        norm2_w = jnp.ones((E,), dtype=jnp.float32)
        mlp_w1 = jax.random.normal(ks[3], (E, 4 * E), dtype=jnp.float32) / np.sqrt(E)
        mlp_b1 = jnp.zeros((4 * E,), dtype=jnp.float32)
        mlp_w2 = jax.random.normal(ks[4], (4 * E, E), dtype=jnp.float32) / np.sqrt(4 * E)
        mlp_b2 = jnp.zeros((E,), dtype=jnp.float32)
        return dict(x=x, qkv_w=qkv_w, qkv_b=qkv_b, out_w=out_w, out_b=out_b, norm1_w=norm1_w, norm2_w=norm2_w, mlp_w1=mlp_w1, mlp_b1=mlp_b1, mlp_w2=mlp_w2, mlp_b2=mlp_b2)
    _L0_attn_in = _L0_attn_setup()

    def _L0_ffn_setup():
        import jax, jax.numpy as jnp
        import numpy as np

        def _bitlinear(x, w_latent):
            scale = jax.lax.stop_gradient(jnp.clip(jnp.mean(jnp.abs(w_latent), axis=1, keepdims=True), 1e-05, None))
            tern = jnp.clip(jnp.round(w_latent / scale), -1.0, 1.0)
            w = w_latent + jax.lax.stop_gradient(tern - w_latent)
            return x @ (w * scale).T
        key = jax.random.key(seed)
        ks = jax.random.split(key, 6)
        dim, hidden, rank = (256, 1024, 16)
        B, S = (4, 1024)
        x = jax.random.normal(ks[0], (B, S, dim), dtype=jnp.float32)
        w_fc = 0.02 * jax.random.normal(ks[1], (hidden, dim), dtype=jnp.float32)
        w_proj = 0.02 * jax.random.normal(ks[2], (dim, hidden), dtype=jnp.float32)
        u = 0.02 * jax.random.normal(ks[3], (hidden, rank), dtype=jnp.float32)
        v = 0.02 * jax.random.normal(ks[4], (rank, dim), dtype=jnp.float32)
        fast_b = jax.random.normal(ks[5], (rank, rank), dtype=jnp.float32)
        gate = jnp.float32(0.05)
        return {'x': x, 'fast_b': fast_b, 'w_fc': w_fc, 'w_proj': w_proj, 'u': u, 'v': v, 'gate': gate}
    _L0_ffn_in = _L0_ffn_setup()
    _d = {'L0_attn_x': _L0_attn_in['x'], 'L0_attn_qkv_w': _L0_attn_in['qkv_w'], 'L0_attn_qkv_b': _L0_attn_in['qkv_b'], 'L0_attn_out_w': _L0_attn_in['out_w'], 'L0_attn_out_b': _L0_attn_in['out_b'], 'L0_attn_norm1_w': _L0_attn_in['norm1_w'], 'L0_attn_norm2_w': _L0_attn_in['norm2_w'], 'L0_attn_mlp_w1': _L0_attn_in['mlp_w1'], 'L0_attn_mlp_b1': _L0_attn_in['mlp_b1'], 'L0_attn_mlp_w2': _L0_attn_in['mlp_w2'], 'L0_attn_mlp_b2': _L0_attn_in['mlp_b2'], 'L0_ffn_fast_b': _L0_ffn_in['fast_b'], 'L0_ffn_w_fc': _L0_ffn_in['w_fc'], 'L0_ffn_w_proj': _L0_ffn_in['w_proj'], 'L0_ffn_u': _L0_ffn_in['u'], 'L0_ffn_v': _L0_ffn_in['v'], 'L0_ffn_gate': _L0_ffn_in['gate']}
    _x0 = _d['L0_attn_x']
    _d['L0_attn_x'] = jax.random.normal(jax.random.fold_in(jax.random.key(seed), 1), (2, 2048, 256), dtype=_x0.dtype)
    del _x0
    return _d

def reference(L0_attn_x, L0_attn_qkv_w, L0_attn_qkv_b, L0_attn_out_w, L0_attn_out_b, L0_attn_norm1_w, L0_attn_norm2_w, L0_attn_mlp_w1, L0_attn_mlp_b1, L0_attn_mlp_w2, L0_attn_mlp_b2, L0_ffn_fast_b, L0_ffn_w_fc, L0_ffn_w_proj, L0_ffn_u, L0_ffn_v, L0_ffn_gate):

    def _L0_attn_ref(x, qkv_w, qkv_b, out_w, out_b, norm1_w, norm2_w, mlp_w1, mlp_b1, mlp_w2, mlp_b2):
        import jax, jax.numpy as jnp
        import numpy as np
        B, L, E, H = (2, 256, 256, 16)
        D = E // H
        EPS = 1e-06

        def rmsnorm(x, w, eps=1e-06):
            var = jnp.mean(jnp.square(x), axis=-1, keepdims=True)
            return x * jax.lax.rsqrt(var + eps) * w

        def cosformer_attn(x, qkv_w, qkv_b, out_w, out_b):
            b, l, e = x.shape
            qkv = x @ qkv_w + qkv_b
            q, k, v = jnp.split(qkv, 3, axis=-1)
            q = q.reshape(b, l, H, D).transpose(0, 2, 1, 3)
            k = k.reshape(b, l, H, D).transpose(0, 2, 1, 3)
            v = v.reshape(b, l, H, D).transpose(0, 2, 1, 3)
            positions = jnp.arange(l, dtype=jnp.float32).reshape(1, 1, l, 1)
            cos_w = jnp.cos(jnp.pi / 2 * positions / l)
            sin_w = jnp.sin(jnp.pi / 2 * positions / l)
            q_prime = jax.nn.relu(q)
            k_prime = jax.nn.relu(k)
            q_cos, q_sin = (q_prime * cos_w, q_prime * sin_w)
            k_cos, k_sin = (k_prime * cos_w, k_prime * sin_w)
            kv_cos_cumsum = jnp.cumsum(jnp.einsum('bhld,bhle->bhlde', k_cos, v), axis=2)
            context_cos = jnp.einsum('bhld,bhlde->bhle', q_cos, kv_cos_cumsum)
            kv_sin_cumsum = jnp.cumsum(jnp.einsum('bhld,bhle->bhlde', k_sin, v), axis=2)
            context_sin = jnp.einsum('bhld,bhlde->bhle', q_sin, kv_sin_cumsum)
            context = context_cos + context_sin
            k_cos_cumsum = jnp.cumsum(k_cos, axis=2)
            k_sin_cumsum = jnp.cumsum(k_sin, axis=2)
            norm = jnp.einsum('bhld,bhld->bhl', q_cos, k_cos_cumsum) + jnp.einsum('bhld,bhld->bhl', q_sin, k_sin_cumsum)
            output = context / (norm[..., None] + EPS)
            output = output.transpose(0, 2, 1, 3).reshape(b, l, e)
            return output @ out_w + out_b
        h = x + cosformer_attn(rmsnorm(x, norm1_w), qkv_w, qkv_b, out_w, out_b)
        m = rmsnorm(h, norm2_w)
        m = jax.nn.gelu(m @ mlp_w1 + mlp_b1) @ mlp_w2 + mlp_b2
        return h + m

    def _L0_ffn_ref(x, fast_b, w_fc, w_proj, u, v, gate):
        import jax, jax.numpy as jnp
        import numpy as np

        def _bitlinear(x, w_latent):
            scale = jax.lax.stop_gradient(jnp.clip(jnp.mean(jnp.abs(w_latent), axis=1, keepdims=True), 1e-05, None))
            tern = jnp.clip(jnp.round(w_latent / scale), -1.0, 1.0)
            w = w_latent + jax.lax.stop_gradient(tern - w_latent)
            return x @ (w * scale).T
        h = _bitlinear(x, w_fc) + gate * (x @ v.T @ fast_b.T @ u.T)
        r = jnp.maximum(h, 0.0)
        return _bitlinear(r * r, w_proj)
    x = L0_attn_x
    xn = _layernorm(x, axis=-1)
    x = x + _L0_attn_ref(xn, L0_attn_qkv_w, L0_attn_qkv_b, L0_attn_out_w, L0_attn_out_b, L0_attn_norm1_w, L0_attn_norm2_w, L0_attn_mlp_w1, L0_attn_mlp_b1, L0_attn_mlp_w2, L0_attn_mlp_b2) + _L0_ffn_ref(xn, L0_ffn_fast_b, L0_ffn_w_fc, L0_ffn_w_proj, L0_ffn_u, L0_ffn_v, L0_ffn_gate)
    return x

_drawn_inputs = setup_inputs


def setup_inputs(seed=0):
    import zlib

    import numpy as np

    out = dict(_drawn_inputs(seed))
    spreads = {'L0_attn_qkv_b': (0.0, 0.329),
     'L0_attn_out_b': (0.0, 0.368),
     'L0_attn_norm1_w': (1.0, 0.6),
     'L0_attn_norm2_w': (1.0, 0.596),
     'L0_attn_mlp_b1': (0.0, 0.638),
     'L0_attn_mlp_b2': (0.0, 0.442)}
    factors = {'L0_ffn_fast_b': 8.0, 'L0_ffn_u': 8.0, 'L0_ffn_v': 8.0}
    for name, (base, spread) in spreads.items():
        noise = np.random.default_rng([zlib.crc32(name.encode()), seed]).standard_normal(out[name].shape)
        drawn = base * np.exp(spread * noise) if base else spread * noise
        out[name] = jnp.asarray(drawn.astype(out[name].dtype))
    for name, factor in factors.items():
        out[name] = (out[name] * factor).astype(out[name].dtype)
    return out
```

```python
from contextlib import ExitStack

import numpy as np

import concourse.bass as bass
from concourse import mybir

F32 = mybir.dt.float32
F32R = mybir.dt.float32r
ALU = mybir.AluOpType
ACT = mybir.ActivationFunctionType
AX_X = mybir.AxisListType.X

P = 128
B, L, E = 2, 2048, 256
H, D = 16, 16
NB = 4
TOK = NB * P
POS = TOK // B
NT = L // POS
KE = E // P
HID = 4 * E
HB = HID // P
VW = D + 1
HW = H // KE * VW
RANK = 16
LN_EPS, RMS_EPS, NORM_EPS = 1e-5, 1e-6, 1e-6

ARENA = 10432
N_SMALL = 11

C_ID, C_MASK, C_DIAG, C_PAR = 0, P, 2 * P, 2 * P + 2 * HW
C_ALL = C_PAR + 2


def constants():
    i = np.arange(P)
    c = np.zeros((P, C_ALL), np.float32)
    c[:, C_ID:C_ID + P] = np.eye(P)
    step = i[None, :] - i[:, None]
    c[:, C_MASK:C_MASK + P] = np.where(step >= 0, np.cos(np.pi / 2 * step / L), 0)
    own = np.repeat((i[:, None] // D == np.arange(H // KE)[None, :]), VW, 1)
    c[:, C_DIAG:C_DIAG + 2 * HW] = np.concatenate([own, own], 1)
    c[:, C_PAR] = i // D % 2 == 0
    c[:, C_PAR + 1] = i // D % 2 == 1
    t = np.zeros((NT, P, 2 * POS + 4), np.float32)
    for n in range(NT):
        a = np.pi / 2 * (n * POS + np.arange(POS)) / L
        t[n, :, 0:POS] = np.cos(a)
        t[n, :, POS:2 * POS] = np.sin(a)
        for k in range(2):
            t[n, :, 2 * POS + k] = np.cos(a[k * P:(k + 1) * P])
            t[n, :, 2 * POS + 2 + k] = np.sin(a[k * P:(k + 1) * P])
    return c, t


def program(nc, x, qkv_w, qkv_b, out_w, out_b, norm1_w, norm2_w, mlp_w1, mlp_b1, mlp_w2, mlp_b2,
            fast_b, w_fc, w_proj, u, v, gate, consts, trig, out):
    with ExitStack() as ctx:
        def sb(name, shape, dt=F32):
            return ctx.enter_context(nc.sbuf_tensor(name, shape, dt))

        def sem(name):
            return ctx.enter_context(nc.semaphore(name))

        wqkv_hi, wqkv_lo = (sb(f"wqkv_{n}", [P, KE, 3 * E], F32R) for n in ("hi", "lo"))
        wo_hi, wo_lo = (sb(f"wo_{n}", [P, KE, E], F32R) for n in ("hi", "lo"))
        w1_hi, w1_lo = (sb(f"w1_{n}", [P, KE, HID], F32R) for n in ("hi", "lo"))
        w2_hi, w2_lo = (sb(f"w2_{n}", [P, HB, E], F32R) for n in ("hi", "lo"))
        fcT = sb("fcT", [P, KE, HID], F32R)
        prT = sb("prT", [P, HB, E], F32R)
        zw_hi, zw_lo = (sb(f"zw_{n}", [P, KE, P], F32R) for n in ("hi", "lo"))
        gT = sb("gT", [P, HID], F32R)
        pr_scale_row = sb("pr_scale_row", [P, E])
        cst = sb("cst", [P, C_ALL])
        ones = sb("ones", [P, P])
        n1w = sb("n1w", [P, KE])
        n2w = sb("n2w", [P, KE])
        qkb = sb("qkb", [P, 2 * KE])
        vb_row = sb("vb_row", [P, E])
        ob_row = sb("ob_row", [P, E])
        b2_row = sb("b2_row", [P, E])
        b1 = sb("b1", [P, HB])
        gate_col = sb("gate_col", [P, 1])
        half = sb("half", [P, NB])

        xin = sb("xin", [P, NB, E])
        tab = sb("tab", [P, 2 * POS + 4])
        xn = sb("xn", [P, NB, E])
        xs = sb("xs", [P, NB, E])
        xb = sb("xb", [P, NB, E])
        res = sb("res", [P, NB, E])
        ctxn = sb("ctxn", [P, NB, E])
        hcur = sb("hcur", [P, NB, E])
        outb = sb("outb", [P, NB, E])
        xT_hi, xT_lo = (sb(f"xT_{n}", [P, KE, TOK], F32R) for n in ("hi", "lo"))
        cT_hi, cT_lo = (sb(f"cT_{n}", [P, KE, TOK], F32R) for n in ("hi", "lo"))
        z_st = sb("z_st", [P, TOK], F32R)
        wide = sb("wide", [P, 2, TOK])
        wide_hi, wide_lo = (sb(f"wide_{n}", [P, 2, TOK], F32R) for n in ("hi", "lo"))
        fc_relu = sb("fc_relu", [P, 2, TOK])
        arena = sb("arena", [P, ARENA])
        at = [0]

        def carve(n):
            at[0] += n
            assert at[0] <= ARENA
            return arena[:, at[0] - n:at[0]]

        qT = carve(KE * TOK).rearrange("p (m n) -> p m n", m=KE)
        kT = carve(KE * TOK).rearrange("p (m n) -> p m n", m=KE)
        q_par = carve(2 * KE * TOK).rearrange("p (r m n) -> p r m n", r=2, m=KE)
        q_trig = carve(2 * KE * TOK).rearrange("p (r m n) -> p r m n", r=2, m=KE)
        k_tok = carve(NB * E).rearrange("p (b n) -> p b n", b=NB)
        v_tok = carve(NB * H * VW).rearrange("p (b h e) -> p b h e", b=NB, h=H)
        v_trig = carve(NB * KE * 2 * HW).rearrange("p (b m r n) -> p b m r n", b=NB, m=KE, r=2)
        raw_at = [0]

        def raw(n):
            raw_at[0] += n
            assert raw_at[0] <= ARENA
            return arena[:, raw_at[0] - n:raw_at[0]]

        raw_fc = raw(HB * E).rearrange("p (m n) -> p m n", m=HB)
        raw_pr = raw(KE * HID).rearrange("p (m n) -> p m n", m=KE)
        raw_qkv = raw(KE * 3 * E).rearrange("p (k n) -> p k n", k=KE)
        raw_wo = raw(KE * E).rearrange("p (k n) -> p k n", k=KE)
        raw_w1 = raw(KE * HID).rearrange("p (k n) -> p k n", k=KE)
        raw_w2 = raw(HB * E).rearrange("p (k n) -> p k n", k=HB)
        less = wide
        u_raw = ctxn[:, 0, 0:HB * RANK].rearrange("p (m r) -> p m r", m=HB)
        v_raw = ctxn[0:RANK, 1, 0:E]
        fbT = ctxn[0:RANK, 2, 0:RANK]
        fb4 = ctxn[0:RANK, 3, 0:P].rearrange("p (q r) -> p q r", q=4)
        u4 = hcur[:, :, :].rearrange("p b n -> p (b n)").rearrange("p (m q r) -> p m q r", m=HB, q=4)
        diag_scale = outb[:, 0, 0:E].rearrange("p (k n) -> p k n", k=KE)
        junk = outb[:, 2:4, :].rearrange("p b n -> p (b n)")
        junk2 = res[:, :, :].rearrange("p b n -> p (b n)")
        sums = sb("sums", [P, HB + KE])
        scales = sb("scales", [P, HB + KE])
        half_pos = sb("half_pos", [P, HB + KE])
        half_neg = sb("half_neg", [P, HB + KE])
        g_by_s = sb("g_by_s", [P, HB])
        weighted = sb("weighted", [P, 4, 4 * P])
        state = sb("state", [P, B, KE, 2 * HW])
        added = sb("added", [P, 2, 2 * HW])
        norm = sb("norm", [P, H])
        recip = sb("recip", [P, H])
        stats = sb("stats", [P, NB, 6])
        mean_sum, mean_dif, var_sum, dif_sq, mean, var = (
            sb(n, [P, NB]) for n in ("mean_sum", "mean_dif", "var_sum", "dif_sq", "mean", "var"))
        var_eps = sb("var_eps", [P, NB])
        rstd = sb("rstd", [P, NB])
        rstd2 = sb("rstd2", [P, NB])
        msq = sb("msq", [P, NB])
        msq_eps = sb("msq_eps", [P, NB])
        rms_eps = sb("rms_eps", [P, NB])
        inv_e = sb("inv_e", [P, NB])
        r1 = sb("r1", [P, NB])
        ssq = sb("ssq", [P, NB])
        ms2 = sb("ms2", [P, NB])
        r2 = sb("r2", [P, NB])

        dense = [ctx.enter_context(nc.psum_tensor(f"dense{i}", [P, TOK], F32)) for i in range(2)]
        shared = [ctx.enter_context(nc.psum_tensor(f"shared{i}", [P, TOK], F32)) for i in range(2)]
        accum = [ctx.enter_context(nc.psum_tensor(f"accum{i}", [P, TOK], F32)) for i in range(2)]
        ctx_ps = ctx.enter_context(nc.psum_tensor("ctx_ps", [P, TOK], F32))
        upd_ps = ctx.enter_context(nc.psum_tensor("upd_ps", [P, TOK], F32))

        ident = cst[:, C_ID:C_ID + P]
        mask = cst[:, C_MASK:C_MASK + P]
        diag = cst[:, C_DIAG:C_DIAG + 2 * HW]

        in_fc, in_pr, in_qkv, in_wo, in_w1, in_w2, in_small, in_const = (
            sem(n) for n in ("in_fc", "in_pr", "in_qkv", "in_wo", "in_w1", "in_w2", "in_small", "in_const"))
        set_mem = sem("set_mem")
        set_act = sem("set_act")
        set_dve = sem("set_dve")
        set_pe = sem("set_pe")
        fb_done, fc_tern, u4_done, pr_tern, diag_done, g_lo_done = (
            sem(n) for n in ("fb_done", "fc_tern", "u4_done", "pr_tern", "diag_done", "g_lo_done"))
        PE_B, PE_FC, PE_G, PE_SC, PE_PR, PE_ALL = 1, 2, 6, 8, 9, 12
        ACT_SUMS, ACT_B, ACT_FC, ACT_G, ACT_SC, ACT_ALL = HB + KE, HB + KE + 1, HB + KE + 2, HB + KE + 6, HB + KE + 8, HB + KE + 12
        DVE_ALL = 30
        x_in = sem("x_in")
        tab_in = sem("tab_in")
        out_sent = sem("out_sent")
        ln_stats = sem("ln_stats")
        ln_pow = sem("ln_pow")
        xn_done = sem("xn_done")
        xb_done = sem("xb_done")
        xs_done = sem("xs_done")
        xnb_done = sem("xnb_done")
        shared_full = sem("shared_full")
        shared_free = sem("shared_free")
        xT_hi_done = sem("xT_hi_done")
        dense_full = sem("dense_full")
        dense_free = sem("dense_free")
        v_trig_done = sem("v_trig_done")
        q_par_done = sem("q_par_done")
        q_trig_done = sem("q_trig_done")
        upd_full = sem("upd_full")
        upd_free = sem("upd_free")
        z_hi_done = sem("z_hi_done")
        k_turned = sem("k_turned")
        k_tok_done = sem("k_tok_done")
        av_done = sem("av_done")
        ctx_full = sem("ctx_full")
        norm_done = sem("norm_done")
        ctx_free = sem("ctx_free")
        upd_used = sem("upd_used")
        relu_done = sem("relu_done")
        wide_done = sem("wide_done")
        hi_done = sem("hi_done")
        lo_even = sem("lo_even")
        lo_odd = sem("lo_odd")
        wide_used = sem("wide_used")
        cT_hi_done = sem("cT_hi_done")
        o_done = sem("o_done")
        ssq_done = sem("ssq_done")
        r2_done = sem("r2_done")
        hs_done = sem("hs_done")
        res_done = sem("res_done")
        ffn_done = sem("ffn_done")
        out_done = sem("out_done")

        N_STATS = NB + 7
        N_SHARED = 26
        S_V, S_SCORE, S_CT, S_OUT, S_HT, S_XT = 0, 2, 18, 20, 22, 24
        N_DENSE = 20
        D_K, D_Q, D_FC, D_MLP = 0, 2, 4, 12
        N_DFREE = D_MLP
        N_UPD = 1 + NB * KE

        def shared_use(t, n):
            return KE + t * N_SHARED + n

        def later(eng, sem_, n):
            if not isinstance(n, int) or n > 0:
                eng.wait_ge(sem_, n)

        def chunk_block(j):
            return (j % B) * 2 + j // B

        block = ctx.enter_context(nc.Block())

        @block.sync
        def _(sp):
            def load_x(t):
                for b in range(B):
                    sp.dma_start(xin[:, 2 * b:2 * b + 2, :],
                                 x[b, bass.ds(t * POS, POS), :].rearrange("(c p) e -> p c e", p=P)).then_inc(x_in, 16)

            def load_tab(t):
                sp.dma_start(tab[:, :], trig[bass.ds(t, 1), :, :].rearrange("a p n -> p (a n)")).then_inc(tab_in, 16)

            sp.dma_start(cst[:, :], consts).then_inc(in_const, 16)
            load_x(0)
            load_tab(0)
            sp.dma_start(raw_fc, w_fc.rearrange("(m p) n -> p m n", p=P)).then_inc(in_fc, 16)
            sp.dma_start(raw_pr, w_proj.rearrange("(m p) n -> p m n", p=P)).then_inc(in_pr, 16)
            sp.dma_start(raw_w1, mlp_w1.rearrange("(k p) n -> p k n", p=P)).then_inc(in_w1, 16)
            sp.dma_start(raw_w2, mlp_w2.rearrange("(k p) n -> p k n", p=P)).then_inc(in_w2, 16)

            def body(t, more):
                if more:
                    sp.wait_ge(xn_done, (t + 1) * NB)
                    sp.wait_ge(xb_done, t + 1)
                    load_x(t + 1)
                    sp.wait_ge(q_trig_done, (t + 1) * 2 * KE)
                    sp.wait_ge(v_trig_done, (t + 1) * 2 * NB * KE)
                    load_tab(t + 1)
                for b in range(B):
                    sp.wait_ge(out_done, t * 2 + b + 1)
                    sp.dma_start(out[b, bass.ds(t * POS, POS), :].rearrange("(c p) e -> p c e", p=P),
                                 outb[:, 2 * b:2 * b + 2, :]).then_inc(out_sent, 16)

            body(0, True)
            with sp.Fori(1, NT - 1) as t:
                body(t, True)
            body(NT - 1, False)
            sp.wait_ge(out_sent, NT * 32)

        @block.gpsimd
        def _(pool):
            pool.memset(half[:, :], -0.5).then_inc(set_mem, 1)
            pool.memset(rms_eps[:, :], RMS_EPS).then_inc(set_mem, 1)
            pool.memset(inv_e[:, :], 1.0 / E).then_inc(set_mem, 1)
            pool.memset(ones[:, :], 1.0).then_inc(set_mem, 1)
            pool.memset(state[:, :, :, :].rearrange("p b k n -> p (b k n)"), 0.0).then_inc(set_mem, 1)
            pool.memset(fb4.rearrange("p q r -> p (q r)"), 0.0).then_inc(set_mem, 1)
            pool.memset(u4.rearrange("p m q r -> p (m q r)"), 0.0).then_inc(set_mem, 1)

            def inverse_root(t):
                pool.wait_ge(ln_stats, t * N_STATS + N_STATS)
                pool.tensor_tensor(rstd[:, :], var_eps[:, :], half[:, :], ALU.pow).then_inc(ln_pow, 1)
                pool.wait_ge(ln_pow, t * 5 + 1)
                pool.tensor_tensor(rstd2[:, :], rstd[:, :], rstd[:, :], ALU.mult).then_inc(ln_pow, 1)
                pool.wait_ge(ln_pow, t * 5 + 2)
                pool.tensor_tensor(msq[:, :], rstd2[:, :], var[:, :], ALU.mult).then_inc(ln_pow, 1)
                pool.wait_ge(ln_pow, t * 5 + 3)
                pool.tensor_tensor(msq_eps[:, :], msq[:, :], rms_eps[:, :], ALU.add).then_inc(ln_pow, 1)
                pool.wait_ge(ln_pow, t * 5 + 4)
                pool.tensor_tensor(r1[:, :], msq_eps[:, :], half[:, :], ALU.pow).then_inc(ln_pow, 1)

            def x_plus_b2(t):
                pool.tensor_tensor(xb[:, :, :], xin[:, :, :],
                                   b2_row[:, :].rearrange("p (a n) -> p a n", a=1).broadcast_to([P, NB, E]),
                                   ALU.add).then_inc(xb_done, 1)

            pool.dma_start(raw_qkv, qkv_w.rearrange("(k p) n -> p k n", p=P)).then_inc(in_qkv, 16)
            pool.dma_start(raw_wo, out_w.rearrange("(k p) n -> p k n", p=P)).then_inc(in_wo, 16)
            pool.wait_ge(set_mem, 7)
            inverse_root(0)
            pool.wait_ge(x_in, 32)
            pool.wait_ge(in_small, 16 * N_SMALL)
            x_plus_b2(0)

            def body(t, more):
                pool.wait_ge(tab_in, t * 16 + 16)
                later(pool, ctx_full, t * NB)
                for m in range(KE):
                    pool.wait_ge(dense_free, t * N_DFREE + D_Q + m + 1)
                    for r in range(2):
                        row = tab[:, r * POS:(r + 1) * POS].rearrange("p (a n) -> p a n", a=1)
                        pool.tensor_tensor(q_trig[:, r, m, :].rearrange("p (b n) -> p b n", b=B),
                                           qT[:, m, :].rearrange("p (b n) -> p b n", b=B),
                                           row.broadcast_to([P, B, POS]), ALU.mult).then_inc(q_trig_done, 1)
                pool.wait_ge(xs_done, (t + 1) * NB)
                pool.wait_ge(xn_done, (t + 1) * NB)
                pool.tensor_tensor(xn[:, :, :], xn[:, :, :],
                                   ob_row[:, :].rearrange("p (a n) -> p a n", a=1).broadcast_to([P, NB, E]),
                                   ALU.add).then_inc(xnb_done, 1)

                def lo_part(n):
                    pool.wait_ge(hi_done, t * 2 * HB + n + 1)
                    pool.tensor_tensor(wide_lo[:, n % 2, :], wide[:, n % 2, :],
                                       wide_hi[:, n % 2, :].bitcast(F32), ALU.subtract).then_inc(lo_odd, 1)

                for j in range(NB):
                    b = j % B
                    if j in (0, 2):
                        lo_part(j + 1)
                    for m in range(KE):
                        n = j * KE + m
                        pool.wait_ge(upd_free, t * N_UPD + 2 + n)
                        pool.wait_ge(ctx_full, t * NB + j + 1)
                        later(pool, upd_used, t * NB * KE + max(n - 3, 0))
                        pool.tensor_tensor(state[:, b, m, :], state[:, b, m, :], added[:, n % 2, :],
                                           ALU.add).then_inc(upd_used, 1)
                lo_part(5)
                pool.wait_ge(ssq_done, (t + 1) * NB)
                pool.tensor_tensor(ms2[:, :], ssq[:, :], inv_e[:, :], ALU.mult).then_inc(r2_done, 1)
                pool.wait_ge(r2_done, t * 3 + 1)
                pool.tensor_tensor(ms2[:, :], ms2[:, :], rms_eps[:, :], ALU.add).then_inc(r2_done, 1)
                pool.wait_ge(r2_done, t * 3 + 2)
                pool.tensor_tensor(r2[:, :], ms2[:, :], half[:, :], ALU.pow).then_inc(r2_done, 1)
                lo_part(7)
                pool.wait_ge(shared_free, shared_use(t, S_OUT + 1) + 1)
                later(pool, out_done, t * 2)
                pool.tensor_tensor(res[:, :, :], xb[:, :, :], hcur[:, :, :], ALU.add).then_inc(res_done, 1)
                pool.wait_ge(ffn_done, (t + 1) * NB)
                pool.wait_ge(res_done, t * 2 + 1)
                pool.tensor_tensor(res[:, :, :], res[:, :, :], ctxn[:, :, :], ALU.add).then_inc(res_done, 1)
                lo_part(9)
                if more:
                    inverse_root(t + 1)
                    pool.wait_ge(x_in, t * 32 + 64)
                lo_part(11)
                lo_part(13)
                if more:
                    x_plus_b2(t + 1)
                lo_part(15)

            body(0, True)
            with pool.Fori(1, NT - 1) as t:
                body(t, True)
            body(NT - 1, False)

        @block.scalar
        def _(act):
            smalls = [
                (b2_row[:, :], mlp_b2.rearrange("(a n) -> a n", a=1).broadcast_to([P, E])),
                (n1w[:, :], norm1_w.rearrange("(k p) -> p k", p=P)),
                (n2w[:, :], norm2_w.rearrange("(k p) -> p k", p=P)),
                (qkb[:, :], qkv_b[0:2 * E].rearrange("(k p) -> p k", p=P)),
                (vb_row[:, :], qkv_b[2 * E:3 * E].rearrange("(a n) -> a n", a=1).broadcast_to([P, E])),
                (ob_row[:, :], out_b.rearrange("(a n) -> a n", a=1).broadcast_to([P, E])),
                (b1[:, :], mlp_b1.rearrange("(k p) -> p k", p=P)),
                (gate_col[:, :], gate.broadcast_to([P, 1])),
                (u_raw, u.rearrange("(m p) r -> p m r", p=P)),
                (v_raw, v),
                (fbT, fast_b.rearrange("r k -> k r")),
            ]
            assert len(smalls) == N_SMALL
            for dst, src in smalls:
                act.dma_start(dst, src, allow_slow_non_contiguous=True).then_inc(in_small, 16)

            n = 0
            for m in range(HB):
                if m == 0:
                    act.wait_ge(in_fc, 16)
                act.activation(junk[:, 0:E], raw_fc[:, m, :], ACT.Abs, accum_out=sums[:, m:m + 1]).then_inc(set_act, 1)
                n += 1
                act.wait_ge(set_act, n)
            act.wait_ge(in_pr, 16)
            for m in range(KE):
                act.activation(junk2, raw_pr[:, m, :], ACT.Abs, accum_out=sums[:, HB + m:HB + m + 1]).then_inc(set_act, 1)
                n += 1
                act.wait_ge(set_act, n)
            def scale_x(t):
                act.wait_ge(ln_pow, t * 5 + 5)
                for k in range(NB):
                    act.wait_ge(xn_done, t * NB + k + 1)
                    act.activation(xs[:, k, :], xn[:, k, :], ACT.Copy, scale=r1[:, k:k + 1]).then_inc(xs_done, 1)

            def x_hi(t):
                for m in range(KE):
                    act.wait_ge(shared_full, shared_use(t, m - KE) + 1)
                    act.activation(xT_hi[:, m, :], shared[m][:, :], ACT.Copy).then_inc(xT_hi_done, 1)

            scale_x(0)
            x_hi(0)
            act.wait_ge(set_pe, PE_B)
            act.activation(zw_hi[:, :, :].rearrange("p k n -> p (k n)"), upd_ps[:, 0:KE * P], ACT.Copy).then_inc(set_act, 1)
            for m in range(KE):
                for g in range(2):
                    act.wait_ge(set_pe, PE_FC + m * 2 + g)
                    act.activation(fcT[:, m, g * TOK:(g + 1) * TOK], (dense + accum)[m * 2 + g][:, :],
                                   ACT.Copy).then_inc(set_act, 1)
            for g in range(2):
                act.wait_ge(set_pe, PE_G + g)
                act.activation(gT[:, g * TOK:(g + 1) * TOK], dense[g][:, :], ACT.Copy).then_inc(set_act, 1)
            act.wait_ge(set_pe, PE_SC)
            act.activation(pr_scale_row[:, :], ctx_ps[:, 0:E], ACT.Copy).then_inc(set_act, 1)
            for g in range(4):
                act.wait_ge(set_pe, PE_PR + g)
                act.activation(prT[:, 2 * g:2 * g + 2, :].rearrange("p h n -> p (h n)"),
                               (dense + accum)[g][:, :], ACT.Copy).then_inc(set_act, 1)
            act.wait_ge(set_dve, DVE_ALL)

            def body(t, more):
                def dense_ready(n):
                    act.wait_ge(dense_full, t * N_DENSE + n + 1)

                for i, (dst, base) in enumerate(((kT, KE), (qT, 0))):
                    for m in range(KE):
                        dense_ready(i * KE + m)
                        if i == 1 and m == 0:
                            later(act, q_trig_done, t * 2 * KE)
                            later(act, q_par_done, t * 2 * KE)
                        act.activation(dst[:, m, :], dense[m][:, :], ACT.Relu,
                                       bias=qkb[:, base + m:base + m + 1]).then_inc(dense_free, 1)
                act.wait_ge(upd_full, t * N_UPD + 1)
                act.activation(z_st[:, :], upd_ps[:, :], ACT.Copy).then_inc(z_hi_done, 1)
                for g in range(2):
                    act.wait_ge(k_turned, t * 2 + g + 1)
                    act.activation(k_tok[:, 2 * g:2 * g + 2, :].rearrange("p b n -> p (b n)"), accum[g][:, :],
                                   ACT.Copy).then_inc(k_tok_done, 1)

                def ffn_block(m):
                    dense_ready(D_FC + m)
                    act.activation(fc_relu[:, m % 2, :], dense[m % 2][:, :], ACT.Relu,
                                   scale=scales[:, m:m + 1]).then_inc(dense_free, 1)
                    later(act, wide_used, t * 2 * HB + max(m - 1, 0))
                    act.wait_ge(dense_free, t * N_DFREE + D_FC + m + 1)
                    act.activation(wide[:, m % 2, :], fc_relu[:, m % 2, :], ACT.Square).then_inc(wide_done, 1)

                def mlp_block(m):
                    dense_ready(D_MLP + m)
                    act.wait_ge(wide_used, t * 2 * HB + HB + m - 1)
                    act.activation(wide[:, m % 2, :], dense[m % 2][:, :], ACT.Gelu_apprx_tanh,
                                   bias=b1[:, m:m + 1]).then_inc(wide_done, 1)
                ffn_block(0)
                act.wait_ge(tab_in, t * 16 + 16)
                for k in range(NB):
                    act.wait_ge(shared_free, shared_use(t, S_V + k // 2) + 1)
                    for m in range(KE):
                        for r in range(2):
                            act.activation(v_trig[:, k, m, r, :],
                                           v_tok[:, k, m * (H // KE):(m + 1) * (H // KE), :].rearrange("p h e -> p (h e)"),
                                           ACT.Copy, scale=tab[:, 2 * POS + 2 * r + k % 2:2 * POS + 2 * r + k % 2 + 1]
                                           ).then_inc(v_trig_done, 1)
                for m in range(1, 6):
                    ffn_block(m)
                for m in range(KE):
                    act.wait_ge(shared_full, shared_use(t, S_CT + m) + 1)
                    act.activation(cT_hi[:, m, :], shared[m][:, :], ACT.Copy).then_inc(cT_hi_done, 1)
                ffn_block(6)
                for k in range(NB):
                    act.wait_ge(shared_free, shared_use(t, S_OUT + k // 2) + 1)
                    later(act, out_sent, t * 32)
                    act.activation(outb[:, k, :], hcur[:, k, :], ACT.Square,
                                   accum_out=ssq[:, k:k + 1]).then_inc(ssq_done, 1)
                ffn_block(7)
                for m in range(KE):
                    act.wait_ge(shared_full, shared_use(t, S_HT + m) + 1)
                    act.activation(cT_hi[:, m, :], shared[m][:, :], ACT.Copy).then_inc(cT_hi_done, 1)
                for m in range(HB):
                    mlp_block(m)
                    if m == 3 and more:
                        scale_x(t + 1)
                    if m == 5 and more:
                        x_hi(t + 1)

            body(0, True)
            with act.Fori(1, NT - 1) as t:
                body(t, True)
            body(NT - 1, False)

        @block.vector
        def _(dve):
            def ln_statistics(t):
                base = t * N_STATS
                dve.wait_ge(x_in, t * 32 + 32)
                later(dve, ln_pow, t * 5)
                for k in range(NB):
                    dve.bn_stats(stats[:, k, :], xin[:, k, :]).then_inc(ln_stats, 1)
                dve.wait_ge(ln_stats, base + NB)
                for dst, col, op in ((mean_sum, 1, ALU.add), (mean_dif, 1, ALU.subtract), (var_sum, 2, ALU.add)):
                    dve.tensor_tensor(dst[:, :], stats[:, :, col], stats[:, :, 3 + col], op).then_inc(ln_stats, 1)
                dve.wait_ge(ln_stats, base + NB + 3)
                dve.scalar_tensor_tensor(dif_sq[:, :], mean_dif[:, :], 0.25, mean_dif[:, :],
                                         ALU.mult, ALU.mult).then_inc(ln_stats, 1)
                dve.tensor_scalar(mean[:, :], mean_sum[:, :], 0.5, None, ALU.mult).then_inc(ln_stats, 1)
                dve.wait_ge(ln_stats, base + NB + 5)
                dve.scalar_tensor_tensor(var[:, :], var_sum[:, :], 1.0 / E, dif_sq[:, :],
                                         ALU.mult, ALU.add).then_inc(ln_stats, 1)
                dve.wait_ge(ln_stats, base + NB + 6)
                dve.tensor_scalar(var_eps[:, :], var[:, :], LN_EPS, None, ALU.add).then_inc(ln_stats, 1)

            def layernorm(t):
                dve.wait_ge(ln_pow, t * 5 + 1)
                for k in range(NB):
                    dve.tensor_scalar(xn[:, k, :], xin[:, k, :], mean[:, k:k + 1], rstd[:, k:k + 1],
                                      ALU.subtract, ALU.mult).then_inc(xn_done, 1)

            def x_lo(t):
                for m in range(KE):
                    dve.wait_ge(xT_hi_done, t * KE + m + 1)
                    dve.tensor_tensor(xT_lo[:, m, :], shared[m][:, :], xT_hi[:, m, :].bitcast(F32),
                                      ALU.subtract).then_inc(shared_free, 1)

            ln_statistics(0)
            layernorm(0)
            dve.wait_ge(in_small, 16 * N_SMALL)
            dve.wait_ge(in_const, 16)
            dve.wait_ge(set_mem, 7)
            dve.tensor_copy(fb4[:, :, 0:RANK], fbT.rearrange("p (a r) -> p a r", a=1).broadcast_to([RANK, 4, RANK])
                            ).then_inc(fb_done, 1)
            n = 0
            x_lo(0)
            for src, load, scale, hi, lo in (
                    (raw_qkv, in_qkv, n1w, wqkv_hi, wqkv_lo), (raw_wo, in_wo, None, wo_hi, wo_lo),
                    (raw_w1, in_w1, n2w, w1_hi, w1_lo), (raw_w2, in_w2, None, w2_hi, w2_lo)):
                dve.wait_ge(load, 16)
                if scale is not None:
                    for k in range(KE):
                        dve.tensor_scalar(src[:, k, :], src[:, k, :], scale[:, k:k + 1], None, ALU.mult).then_inc(set_dve, 1)
                        n += 1
                    dve.wait_ge(set_dve, n)
                dve.tensor_copy(hi[:, :, :], src).then_inc(set_dve, 1)
                n += 1
                dve.wait_ge(set_dve, n)
                dve.tensor_tensor(lo[:, :, :], src, hi[:, :, :].bitcast(F32), ALU.subtract).then_inc(set_dve, 1)
                n += 1
            dve.wait_ge(set_act, ACT_SUMS)
            for lo_c, hi_c, count in ((0, HB, E), (HB, HB + KE, HID)):
                dve.tensor_scalar(scales[:, lo_c:hi_c], sums[:, lo_c:hi_c], 1.0 / count, 1e-5,
                                  ALU.mult, ALU.max).then_inc(set_dve, 1)
                n += 1
            dve.wait_ge(set_dve, n)
            dve.tensor_scalar(half_pos[:, :], scales[:, :], 0.5, None, ALU.mult).then_inc(set_dve, 1)
            dve.tensor_scalar(half_neg[:, :], scales[:, :], -0.5, None, ALU.mult).then_inc(set_dve, 1)
            dve.reciprocal(g_by_s[:, :], scales[:, 0:HB]).then_inc(set_dve, 1)
            n += 3
            for m in range(HB):
                dve.wait_ge(set_dve, n)
                dve.tensor_scalar(less[:, m % 2, 0:E], raw_fc[:, m, :], half_neg[:, m:m + 1], None,
                                  ALU.is_lt).then_inc(set_dve, 1)
                n += 1
                dve.wait_ge(set_dve, n)
                dve.scalar_tensor_tensor(raw_fc[:, m, :], raw_fc[:, m, :], half_pos[:, m:m + 1], less[:, m % 2, 0:E],
                                         ALU.is_gt, ALU.subtract).then_inc(fc_tern, 1)
            dve.tensor_scalar(g_by_s[:, :], g_by_s[:, :], gate_col[:, 0:1], None, ALU.mult).then_inc(set_dve, 1)
            n += 1
            dve.wait_ge(set_dve, n)
            for q in range(4):
                dve.tensor_tensor(u4[:, :, q, 0:RANK], u_raw,
                                  g_by_s[:, :].rearrange("p (m a) -> p m a", a=1).broadcast_to([P, HB, RANK]),
                                  ALU.mult).then_inc(u4_done, 1)
            dve.wait_ge(fc_tern, HB)
            for m in range(KE):
                both = less[:, :, :].rearrange("p a n -> p (a n)")
                c = HB + m
                dve.wait_ge(pr_tern, m)
                dve.tensor_scalar(both, raw_pr[:, m, :], half_neg[:, c:c + 1], None, ALU.is_lt).then_inc(set_dve, 1)
                n += 1
                dve.wait_ge(set_dve, n)
                dve.scalar_tensor_tensor(raw_pr[:, m, :], raw_pr[:, m, :], half_pos[:, c:c + 1], both,
                                         ALU.is_gt, ALU.subtract).then_inc(pr_tern, 1)
                dve.tensor_scalar(diag_scale[:, m, :], ident, scales[:, c:c + 1], None, ALU.mult).then_inc(diag_done, 1)
            dve.wait_ge(set_act, ACT_B)
            dve.tensor_tensor(zw_lo[:, :, :].rearrange("p k n -> p (k n)"), upd_ps[:, 0:KE * P],
                              zw_hi[:, :, :].rearrange("p k n -> p (k n)").bitcast(F32), ALU.subtract).then_inc(set_dve, 1)
            n += 1
            for g in range(2):
                dve.wait_ge(set_act, ACT_G + g)
                for r in (32, 96):
                    part = gT[r:r + 32, g * TOK:(g + 1) * TOK]
                    dve.tensor_tensor(part, dense[g][r:r + 32, :], part.bitcast(F32), ALU.subtract).then_inc(g_lo_done, 1)
            dve.wait_ge(set_dve, n)
            dve.wait_ge(set_pe, PE_ALL)
            dve.memset(v_tok[:, :, :, D:VW].rearrange("p b h e -> p (b h) e"), 1.0).then_inc(set_dve, 1)
            n += 1
            assert n == DVE_ALL, n

            def body(t, more):
                later(dve, v_trig_done, t * 2 * NB * KE)
                for g in range(2):
                    dve.wait_ge(shared_full, shared_use(t, S_V + g) + 1)
                    for_block = shared[g][:, :].rearrange("p (b h e) -> p b h e", b=2, h=H)
                    bias = vb_row[:, :].rearrange("p (a h e) -> p a h e", a=1, h=H).broadcast_to([P, 2, H, D])
                    dve.tensor_tensor(v_tok[:, 2 * g:2 * g + 2, :, 0:D], for_block, bias, ALU.add).then_inc(shared_free, 1)
                for m in range(KE):
                    dve.wait_ge(dense_free, t * N_DFREE + D_Q + m + 1)
                    for r in range(2):
                        dve.tensor_scalar(q_par[:, r, m, :], qT[:, m, :], cst[:, C_PAR + r:C_PAR + r + 1], None,
                                          ALU.mult).then_inc(q_par_done, 1)
                dve.wait_ge(z_hi_done, t + 1)
                dve.tensor_tensor(z_st[64:128, :], upd_ps[64:128, :], z_st[64:128, :].bitcast(F32),
                                  ALU.subtract).then_inc(upd_free, 1)

                def split(n):
                    dve.wait_ge(wide_done, t * 2 * HB + n + 1)
                    dve.tensor_copy(wide_hi[:, n % 2, :], wide[:, n % 2, :]).then_inc(hi_done, 1)
                    if n % 2 == 0:
                        dve.wait_ge(hi_done, t * 2 * HB + n + 1)
                        dve.tensor_tensor(wide_lo[:, n % 2, :], wide[:, n % 2, :], wide_hi[:, n % 2, :].bitcast(F32),
                                          ALU.subtract).then_inc(lo_even, 1)

                def weigh(j, g):
                    i = 4 * j + g
                    dve.wait_ge(shared_full, shared_use(t, S_SCORE + i) + 1)
                    later(dve, av_done, t * 4 * NB + max(i - 3, 0))
                    dve.tensor_tensor(weighted[:, g, :].rearrange("p (a n) -> p a n", a=4),
                                      shared[g % 2][:, :].rearrange("p (a n) -> p a n", a=4),
                                      mask.rearrange("p (a n) -> p a n", a=1).broadcast_to([P, 4, P]),
                                      ALU.mult).then_inc(shared_free, 1)

                def context(j):
                    heads = ctx_ps[:, 0:H * VW].rearrange("p (h e) -> p h e", e=VW)
                    c = t * 2 * NB + 2 * j
                    dve.wait_ge(ctx_full, t * NB + j + 1)
                    dve.tensor_scalar(norm[:, :], heads[:, :, D], NORM_EPS, None, ALU.add).then_inc(norm_done, 1)
                    dve.wait_ge(norm_done, c + 1)
                    dve.reciprocal(recip[:, :], norm[:, :]).then_inc(norm_done, 1)
                    dve.wait_ge(norm_done, c + 2)
                    if j == 0:
                        later(dve, res_done, t * 2)
                    dve.tensor_tensor(ctxn[:, chunk_block(j), :].rearrange("p (h e) -> p h e", e=D), heads[:, :, 0:D],
                                      recip[:, :].rearrange("p (h a) -> p h a", a=1).broadcast_to([P, H, D]),
                                      ALU.mult).then_inc(ctx_free, 1)

                split(0)
                for j in range(NB):
                    weigh(j, 0)
                    weigh(j, 1)
                    split(j + 1)
                    weigh(j, 2)
                    weigh(j, 3)
                    context(j)
                    for m in range(KE):
                        n = j * KE + m
                        dve.wait_ge(upd_full, t * N_UPD + 2 + n)
                        later(dve, upd_used, t * NB * KE + max(n - 1, 0))
                        dve.tensor_tensor(added[:, n % 2, :], upd_ps[:, 0:2 * HW], diag, ALU.mult).then_inc(upd_free, 1)
                for m in range(KE):
                    dve.wait_ge(cT_hi_done, t * 2 * KE + m + 1)
                    dve.tensor_tensor(cT_lo[:, m, :], shared[m][:, :], cT_hi[:, m, :].bitcast(F32),
                                      ALU.subtract).then_inc(shared_free, 1)
                split(5)
                dve.wait_ge(xnb_done, t + 1)
                for g in range(2):
                    dve.wait_ge(shared_full, shared_use(t, S_OUT + g) + 1)
                    dve.tensor_tensor(hcur[:, 2 * g:2 * g + 2, :].rearrange("p b n -> p (b n)"), shared[g][:, :],
                                      xn[:, 2 * g:2 * g + 2, :].rearrange("p b n -> p (b n)"), ALU.add).then_inc(shared_free, 1)
                split(6)
                dve.wait_ge(r2_done, t * 3 + 3)
                for k in range(NB):
                    dve.tensor_scalar(xs[:, k, :], hcur[:, k, :], r2[:, k:k + 1], None, ALU.mult).then_inc(hs_done, 1)
                split(7)
                for m in range(KE):
                    dve.wait_ge(cT_hi_done, t * 2 * KE + KE + m + 1)
                    dve.tensor_tensor(cT_lo[:, m, :], shared[m][:, :], cT_hi[:, m, :].bitcast(F32),
                                      ALU.subtract).then_inc(shared_free, 1)
                dve.wait_ge(wide_used, t * 2 * HB + HB)
                for k in range(NB):
                    dve.scalar_tensor_tensor(ctxn[:, k, :], accum[k // 2][:, (k % 2) * E:(k % 2 + 1) * E],
                                             msq_eps[:, k:k + 1], pr_scale_row[:, :],
                                             ALU.mult, ALU.mult).then_inc(ffn_done, 1)
                split(8)
                if more:
                    ln_statistics(t + 1)
                split(9)
                split(10)
                if more:
                    layernorm(t + 1)
                split(11)
                split(12)
                split(13)
                if more:
                    x_lo(t + 1)
                split(14)
                split(15)
                dve.wait_ge(res_done, t * 2 + 2)
                later(dve, out_sent, t * 32)
                dve.wait_ge(wide_used, (t + 1) * 2 * HB)
                for g in range(2):
                    dve.tensor_tensor(outb[:, 2 * g:2 * g + 2, :].rearrange("p b n -> p (b n)"), accum[g][:, :],
                                      res[:, 2 * g:2 * g + 2, :].rearrange("p b n -> p (b n)"), ALU.add).then_inc(out_done, 1)

            body(0, True)
            with dve.Fori(1, NT - 1) as t:
                body(t, True)
            body(NT - 1, False)

        @block.tensor
        def _(pe):
            def turn_x(t):
                pe.wait_ge(xs_done, (t + 1) * NB)
                for m in range(KE):
                    use = shared_use(t, m - KE)
                    if not isinstance(t, int) or t:
                        pe.wait_ge(shared_free, use - 1)
                    for k in range(NB):
                        mm = pe.transpose(shared[m][:, k * P:(k + 1) * P], xs[:, k, m * P:(m + 1) * P], ident)
                    mm.then_inc(shared_full, 1)

            pe.wait_ge(in_const, 16)
            turn_x(0)
            pe.wait_ge(fb_done, 1)
            for m in range(KE):
                mm = pe.matmul(upd_ps[:, m * P:(m + 1) * P], v_raw[:, m * P:(m + 1) * P],
                               fb4.rearrange("p q r -> p (q r)"), start=True, stop=True)
            mm.then_inc(set_pe, 1)
            pe.wait_ge(fc_tern, HB)
            for m in range(KE):
                for g in range(2):
                    for i in range(4):
                        mm = pe.transpose((dense + accum)[m * 2 + g][:, i * P:(i + 1) * P],
                                          raw_fc[:, 4 * g + i, m * P:(m + 1) * P], ident)
                    mm.then_inc(set_pe, 1)
            pe.wait_ge(u4_done, 4)
            pe.wait_ge(set_act, ACT_FC + 1)
            for g in range(2):
                for i in range(4):
                    mm = pe.transpose(dense[g][:, i * P:(i + 1) * P],
                                      u4[:, 4 * g + i, :, :].rearrange("p q r -> p (q r)"), ident)
                mm.then_inc(set_pe, 1)
            pe.wait_ge(diag_done, KE)
            pe.matmul(ctx_ps[:, 0:E], ones[:, :], diag_scale.rearrange("p k n -> p (k n)"),
                      start=True, stop=True).then_inc(set_pe, 1)
            pe.wait_ge(pr_tern, KE)
            pe.wait_ge(g_lo_done, 4)
            pe.wait_ge(set_act, ACT_G + 1)
            for g in range(4):
                for hb in range(2):
                    for m in range(KE):
                        mm = pe.transpose((dense + accum)[g][:, hb * E + m * P:hb * E + (m + 1) * P],
                                          raw_pr[:, m, (2 * g + hb) * P:(2 * g + hb + 1) * P], ident)
                mm.then_inc(set_pe, 1)
            pe.wait_ge(set_act, ACT_ALL)
            pe.wait_ge(set_dve, DVE_ALL)

            def body(t, more):
                def dense_bank(n):
                    if n < 2:
                        later(pe, wide_done, t * 2 * HB)
                    elif n < D_MLP + 2:
                        later(pe, dense_free, t * N_DFREE + n - 1)
                    else:
                        later(pe, wide_done, t * 2 * HB + HB + n - D_MLP - 1)
                    return dense[n % 2]

                def shared_bank(n):
                    pe.wait_ge(shared_free, shared_use(t, n) - 1)
                    return shared[n % 2]

                def product3(dst, w_hi, w_lo, a_hi, a_lo, cols):
                    for k in range(KE):
                        for i, (w, a) in enumerate(((w_hi, a_hi), (w_hi, a_lo), (w_lo, a_hi))):
                            mm = pe.matmul(dst, w[:, k, cols], a[:, k, :], start=(k == 0 and i == 0),
                                           stop=(k == KE - 1 and i == 2))
                    return mm

                pe.wait_ge(shared_free, shared_use(t, -1) + 1)
                for n, base in ((D_K, E), (D_K + 1, E + P), (D_Q, 0), (D_Q + 1, P)):
                    bank = dense_bank(n)
                    product3(bank[:, :], wqkv_hi, wqkv_lo, xT_hi, xT_lo,
                             slice(base, base + P)).then_inc(dense_full, 1)
                for g in range(2):
                    bank = shared_bank(S_V + g)
                    for i in range(2):
                        tok = slice((2 * g + i) * P, (2 * g + i + 1) * P)
                        for k in range(KE):
                            for c, (a, w) in enumerate(((xT_hi, wqkv_hi), (xT_hi, wqkv_lo), (xT_lo, wqkv_hi))):
                                mm = pe.matmul(bank[:, i * E:(i + 1) * E], a[:, k, tok], w[:, k, 2 * E:3 * E],
                                               start=(k == 0 and c == 0), stop=(k == KE - 1 and c == 2))
                    mm.then_inc(shared_full, 1)
                later(pe, upd_free, t * N_UPD)
                product3(upd_ps[:, :], zw_hi, zw_lo, xT_hi, xT_lo, slice(0, P)).then_inc(upd_full, 1)
                later(pe, out_done, t * 2)
                pe.wait_ge(dense_free, t * N_DFREE + D_K + KE)
                for g in range(2):
                    for i in range(2):
                        for m in range(KE):
                            mm = pe.transpose(accum[g][:, i * E + m * P:i * E + (m + 1) * P],
                                              kT[:, m, (2 * g + i) * P:(2 * g + i + 1) * P], ident)
                    mm.then_inc(k_turned, 1)

                def ffn_up(m):
                    bank = dense_bank(D_FC + m)
                    cols = slice(m * P, (m + 1) * P)
                    for k in range(KE):
                        for i, a in enumerate((xT_hi, xT_lo)):
                            pe.matmul(bank[:, :], fcT[:, k, cols], a[:, k, :], start=(k == 0 and i == 0), stop=False)
                    if m == 0:
                        pe.wait_ge(upd_free, t * N_UPD + 1)
                    pe.matmul(bank[:, :], gT[:, cols], z_st[:, :], start=False, stop=True).then_inc(dense_full, 1)

                def down(n, pairs):
                    first, last = n % HB == 0, n % HB == HB - 1
                    pe.wait_ge(hi_done, t * 2 * HB + n + 1)
                    pe.wait_ge(lo_odd if n % 2 else lo_even, t * HB + n // 2 + 1)
                    for k in range(NB):
                        tok = slice(k * P, (k + 1) * P)
                        for i, (a, w) in enumerate(pairs):
                            mm = pe.matmul(accum[k // 2][:, (k % 2) * E:(k % 2 + 1) * E], a[:, n % 2, tok],
                                           w[:, n % HB, :], start=(first and i == 0 and k % 2 == 0),
                                           stop=(last and i == len(pairs) - 1), skip_group_check=True)
                    mm.then_inc(wide_used, 1)
                    return mm

                def ffn_down(m):
                    if m == 0:
                        pe.wait_ge(k_tok_done, t * 2 + 2)
                    down(m, ((wide_hi, prT), (wide_lo, prT)))

                def scores(j, g):
                    bank = shared_bank(S_SCORE + 4 * j + g)
                    tok = slice(chunk_block(j) * P, (chunk_block(j) + 1) * P)
                    rows = slice(32 * g, 32 * g + 32)
                    if j == 0 and g == 0:
                        pe.wait_ge(q_par_done, (t + 1) * 2 * KE)
                    for m in range(KE):
                        for r in range(2):
                            i = 2 * m + r
                            mm = pe.matmul(bank[:, i * P:(i + 1) * P], kT[rows, m, tok], q_par[rows, r, m, tok],
                                           start=True, stop=True)
                    mm.then_inc(shared_full, 1)

                def within(j, g):
                    k = chunk_block(j)
                    if g == 0:
                        later(pe, ctx_free, t * NB + j)
                    pe.wait_ge(shared_free, shared_use(t, S_SCORE + 4 * j + g) + 1)
                    for m in range(KE):
                        for r in range(2):
                            h = m * (H // KE) + 2 * g + r
                            i = 2 * m + r
                            mm = pe.matmul(ctx_ps[:, h * VW:(h + 1) * VW], weighted[:, g, i * P:(i + 1) * P],
                                           v_tok[:, k, h, :], start=(g == 0 and i == 0), stop=False,
                                           skip_group_check=True)
                    mm.then_inc(av_done, 1)

                def across(j):
                    k = chunk_block(j)
                    pe.wait_ge(q_trig_done, (t + 1) * 2 * KE)
                    later(pe, upd_used, t * NB * KE + max(j - 1, 0) * KE)
                    for m in range(KE):
                        for r in range(2):
                            mm = pe.matmul(ctx_ps[:, m * HW:(m + 1) * HW], q_trig[:, r, m, k * P:(k + 1) * P],
                                           state[:, j % B, m, r * HW:(r + 1) * HW], start=False,
                                           stop=(m == KE - 1 and r == 1), skip_group_check=True)
                    mm.then_inc(ctx_full, 1)

                def update(j, m):
                    k = chunk_block(j)
                    pe.wait_ge(upd_free, t * N_UPD + 1 + j * KE + m)
                    if j == 0:
                        pe.wait_ge(k_tok_done, t * 2 + 2)
                        pe.wait_ge(v_trig_done, (t + 1) * 2 * NB * KE)
                    pe.matmul(upd_ps[:, 0:2 * HW], k_tok[:, k, m * P:(m + 1) * P],
                              v_trig[:, k, m, :, :].rearrange("p r n -> p (r n)"),
                              start=True, stop=True).then_inc(upd_full, 1)

                ffn_up(0)
                ffn_up(1)
                for j in range(NB):
                    scores(j, 0)
                    scores(j, 1)
                    ffn_down(j)
                    scores(j, 2)
                    scores(j, 3)
                    within(j, 0)
                    within(j, 1)
                    ffn_up(j + 2)
                    within(j, 2)
                    within(j, 3)
                    across(j)
                    for m in range(KE):
                        update(j, m)
                pe.wait_ge(ctx_free, t * NB + NB)
                for m in range(KE):
                    bank = shared_bank(S_CT + m)
                    for k in range(NB):
                        mm = pe.transpose(bank[:, k * P:(k + 1) * P], ctxn[:, k, m * P:(m + 1) * P], ident)
                    mm.then_inc(shared_full, 1)
                ffn_down(4)
                ffn_up(6)
                pe.wait_ge(shared_free, shared_use(t, S_CT + 1) + 1)
                for g in range(2):
                    bank = shared_bank(S_OUT + g)
                    for i in range(2):
                        tok = slice((2 * g + i) * P, (2 * g + i + 1) * P)
                        for k in range(KE):
                            for c, (a, w) in enumerate(((cT_hi, wo_hi), (cT_hi, wo_lo), (cT_lo, wo_hi))):
                                mm = pe.matmul(bank[:, i * E:(i + 1) * E], a[:, k, tok], w[:, k, :],
                                               start=(k == 0 and c == 0), stop=(k == KE - 1 and c == 2))
                    mm.then_inc(shared_full, 1)
                ffn_down(5)
                ffn_up(7)
                ffn_down(6)
                ffn_down(7)
                pe.wait_ge(hs_done, (t + 1) * NB)
                for m in range(KE):
                    bank = shared_bank(S_HT + m)
                    for k in range(NB):
                        mm = pe.transpose(bank[:, k * P:(k + 1) * P], xs[:, k, m * P:(m + 1) * P], ident)
                    mm.then_inc(shared_full, 1)

                def mlp_up(m):
                    bank = dense_bank(D_MLP + m)
                    if m == 0:
                        pe.wait_ge(shared_free, shared_use(t, S_HT + 1) + 1)
                    product3(bank[:, :], w1_hi, w1_lo, cT_hi, cT_lo, slice(m * P, (m + 1) * P)).then_inc(dense_full, 1)

                def mlp_down(m):
                    if m == 0:
                        pe.wait_ge(ffn_done, (t + 1) * NB)
                    down(HB + m, ((wide_hi, w2_hi), (wide_hi, w2_lo), (wide_lo, w2_hi)))

                mlp_up(0)
                for m in range(1, HB):
                    mlp_up(m)
                    mlp_down(m - 1)
                    if m == 5 and more:
                        turn_x(t + 1)
                mlp_down(HB - 1)

            body(0, True)
            with pe.Fori(1, NT - 1) as t:
                body(t, True)
            body(NT - 1, False)


_INS = ["x", "qkv_w", "qkv_b", "out_w", "out_b", "norm1_w", "norm2_w", "mlp_w1", "mlp_b1", "mlp_w2", "mlp_b2"]
_FFN_INS = ["fast_b", "w_fc", "w_proj", "u", "v", "gate"]


def kernel(**inputs):
    import concourse.bacc as bacc
    from concourse.bass_utils import run_bass_kernel_spmd

    nc = bacc.Bacc("TRN2", target_bir_lowering=False, num_devices=1)
    arrays, args = {}, []
    for name in ["L0_attn_" + n for n in _INS] + ["L0_ffn_" + n for n in _FFN_INS]:
        a = np.ascontiguousarray(inputs[name])
        if a.ndim == 0:
            a = a.reshape(1, 1)
        arrays[name] = a
        args.append(nc.dram_tensor(name, a.shape, mybir.dt.from_np(a.dtype), kind="ExternalInput").ap())
    for name, a in zip(("consts", "trig"), constants()):
        arrays[name] = a
        args.append(nc.dram_tensor(name, a.shape, F32, kind="ExternalInput").ap())
    args.append(nc.dram_tensor("out", (B, L, E), F32, kind="ExternalOutput").ap())
    program(nc, *args)
    r = run_bass_kernel_spmd(nc, [arrays], core_ids=[0])
    return r.results[0]["out"]
```

```python
from contextlib import ExitStack

import numpy as np

import concourse.bass as bass
from concourse import mybir

F32 = mybir.dt.float32
F32R = mybir.dt.float32r
ALU = mybir.AluOpType
ACT = mybir.ActivationFunctionType
AX_X = mybir.AxisListType.X

P = 128
B, L, E = 2, 2048, 256
H, D = 16, 16
NB = 4
TOK = NB * P
POS = TOK // B
NT = L // POS
KE = E // P
HID = 4 * E
HB = HID // P
VW = D + 1
HW = H // KE * VW
RANK = 16
LN_EPS, RMS_EPS, NORM_EPS = 1e-5, 1e-6, 1e-6

PAIRS = H // 2
PARTS = 3
N_STACK = 4 * PARTS * (1 + 2)
N_SMALL = 11

C_ID, C_MASK, C_DIAG = 0, P, 2 * P
C_ALL = C_DIAG + 2 * HW


def constants():
    i = np.arange(P)
    c = np.zeros((P, C_ALL), np.float32)
    c[:, C_ID:C_ID + P] = np.eye(P)
    step = i[None, :] - i[:, None]
    c[:, C_MASK:C_MASK + P] = np.where(step >= 0, np.cos(np.pi / 2 * step / L), 0)
    own = np.repeat((i[:, None] // D == np.arange(H // KE)[None, :]), VW, 1)
    c[:, C_DIAG:C_DIAG + 2 * HW] = np.concatenate([own, own], 1)
    t = np.zeros((NT, P, 2 * POS + 4), np.float32)
    for n in range(NT):
        a = np.pi / 2 * (n * POS + np.arange(POS)) / L
        t[n, :, 0:POS] = np.cos(a)
        t[n, :, POS:2 * POS] = np.sin(a)
        for k in range(2):
            t[n, :, 2 * POS + k] = np.cos(a[k * P:(k + 1) * P])
            t[n, :, 2 * POS + 2 + k] = np.sin(a[k * P:(k + 1) * P])
    return c, t


def program(nc, x, qkv_w, qkv_b, out_w, out_b, norm1_w, norm2_w, mlp_w1, mlp_b1, mlp_w2, mlp_b2,
            fast_b, w_fc, w_proj, u, v, gate, consts, trig, out):
    with ExitStack() as ctx:
        def sb(name, shape, dt=F32):
            return ctx.enter_context(nc.sbuf_tensor(name, shape, dt))

        def sem(name):
            return ctx.enter_context(nc.semaphore(name))

        wqkv_hi, wqkv_lo = (sb(f"wqkv_{n}", [P, KE, 3 * E], F32R) for n in ("hi", "lo"))
        wo_hi, wo_lo = (sb(f"wo_{n}", [P, KE, E], F32R) for n in ("hi", "lo"))
        w1_hi, w1_lo = (sb(f"w1_{n}", [P, KE, HID], F32R) for n in ("hi", "lo"))
        w2_hi, w2_lo = (sb(f"w2_{n}", [P, HB, E], F32R) for n in ("hi", "lo"))
        fcT = sb("fcT", [P, KE, HID], F32R)
        prT = sb("prT", [P, HB, E], F32R)
        zw_hi, zw_lo = (sb(f"zw_{n}", [P, KE, P], F32R) for n in ("hi", "lo"))
        gT = sb("gT", [P, HID], F32R)
        pr_scale_row = sb("pr_scale_row", [P, E])
        cst = sb("cst", [P, C_ALL])
        ones = sb("ones", [P, P])
        n1w = sb("n1w", [P, KE])
        n2w = sb("n2w", [P, KE])
        qkb = sb("qkb", [P, 2 * KE])
        vb_row = sb("vb_row", [P, E])
        ob_row = sb("ob_row", [P, E])
        b2_row = sb("b2_row", [P, E])
        b1 = sb("b1", [P, HB])
        gate_col = sb("gate_col", [P, 1])
        half = sb("half", [P, NB])

        xin = sb("xin", [P, NB, E])
        tab = sb("tab", [P, 2 * POS + 4])
        xn = sb("xn", [P, NB, E])
        xs = sb("xs", [P, NB, E])
        xb = sb("xb", [P, NB, E])
        late = sb("late", [P, 2, NB, E])
        res = late[:, 0, :, :]
        ctxn = late[:, 1, :, :]
        xT_hi, xT_lo = (sb(f"xT_{n}", [P, KE, TOK], F32R) for n in ("hi", "lo"))
        cT_hi, cT_lo = (sb(f"cT_{n}", [P, KE, TOK], F32R) for n in ("hi", "lo"))
        z_st = sb("z_st", [P, TOK], F32R)
        wide = sb("wide", [P, 2, TOK])
        wide_hi, wide_lo = (sb(f"wide_{n}", [P, 2, TOK], F32R) for n in ("hi", "lo"))
        k_stack = sb("k_stack", [P, 4, KE, TOK], F32R)
        q_stack = sb("q_stack", [P, 4, 2, KE, TOK], F32R)
        arena_words = 6272
        arena = sb("arena", [P, arena_words])
        weighted = sb("weighted", [P, 4, 4 * P])
        at = [0, 0]

        def carve(n, which=0):
            at[which] += n
            assert at[which] <= arena_words
            return arena[:, at[which] - n:at[which]]

        qT = carve(KE * TOK).rearrange("p (m n) -> p m n", m=KE)
        kT = carve(KE * TOK).rearrange("p (m n) -> p m n", m=KE)
        k_tok = carve(NB * E).rearrange("p (b n) -> p b n", b=NB)
        v_tok = carve(NB * H * VW).rearrange("p (b h e) -> p b h e", b=NB, h=H)
        ring = carve(2 * KE * 2 * P + 2 * KE * 2 * HW)
        q_trig = ring[:, 0:2 * KE * 2 * P].rearrange("p (s r m n) -> p s r m n", s=2, r=2, m=KE)
        v_trig = ring[:, 2 * KE * 2 * P:].rearrange("p (s m r n) -> p s m r n", s=2, m=KE, r=2)
        k_parts = weighted[:, :, :].rearrange("p g n -> p (g n)").rearrange("p (i m n) -> p i m n", i=2, m=KE)
        q_parts = ring[:, 0:2 * KE * TOK].rearrange("p (i m n) -> p i m n", i=2, m=KE)

        raw_fc = carve(HB * E, 1).rearrange("p (m n) -> p m n", m=HB)
        raw_pr = carve(KE * HID, 1).rearrange("p (m n) -> p m n", m=KE)
        raw_qkv = carve(KE * 3 * E, 1).rearrange("p (k n) -> p k n", k=KE)
        raw_wo = carve(KE * E, 1).rearrange("p (k n) -> p k n", k=KE)
        u_raw = carve(HB * RANK, 1).rearrange("p (m r) -> p m r", m=HB)
        raw_late = late[:, :, :, :].rearrange("p a b n -> p (a b n)")
        raw_w1 = raw_late.rearrange("p (k n) -> p k n", k=KE)
        raw_w2 = raw_late.rearrange("p (k n) -> p k n", k=HB)
        less = weighted[:, 0:2, :]
        diag_scale = weighted[:, 2, 0:E].rearrange("p (k n) -> p k n", k=KE)
        added = sb("added", [P, 2, 2 * HW])
        added_flat = added[:, :, :].rearrange("p a n -> p (a n)")
        v_raw = added_flat[0:RANK, 0:E]
        fbT = added_flat[0:RANK, E:E + RANK]
        fb4 = added_flat[0:RANK, E + RANK:E + RANK + P].rearrange("p (q r) -> p q r", q=4)
        u4 = wide[:, :, :].rearrange("p a n -> p (a n)").rearrange("p (m q r) -> p m q r", m=HB, q=4)
        junk = xb[:, :, :].rearrange("p b n -> p (b n)")
        sums = sb("sums", [P, HB + KE])
        scales = sb("scales", [P, HB + KE])
        half_pos = sb("half_pos", [P, HB + KE])
        half_neg = sb("half_neg", [P, HB + KE])
        g_by_s = sb("g_by_s", [P, HB])
        state = sb("state", [P, B, KE, 2 * HW])
        norm = sb("norm", [P, H])
        recip = sb("recip", [P, H])
        stats = sb("stats", [P, NB, 6])
        mean_sum, mean_dif, var_sum, dif_sq, mean, var = (
            sb(n, [P, NB]) for n in ("mean_sum", "mean_dif", "var_sum", "dif_sq", "mean", "var"))
        var_eps = sb("var_eps", [P, NB])
        rstd = sb("rstd", [P, NB])
        rstd2 = sb("rstd2", [P, NB])
        msq = sb("msq", [P, NB])
        r1_sq_inv = sb("r1_sq_inv", [P, NB])
        msq_eps = sb("msq_eps", [P, NB])
        rms_eps = sb("rms_eps", [P, NB])
        inv_e = sb("inv_e", [P, NB])
        r1 = sb("r1", [P, NB])
        ssq = sb("ssq", [P, NB])
        ms2 = sb("ms2", [P, NB])
        r2 = sb("r2", [P, NB])

        dense = [ctx.enter_context(nc.psum_tensor(f"dense{i}", [P, TOK], F32)) for i in range(2)]
        shared = [ctx.enter_context(nc.psum_tensor(f"shared{i}", [P, TOK], F32)) for i in range(2)]
        accum = [ctx.enter_context(nc.psum_tensor(f"accum{i}", [P, TOK], F32)) for i in range(2)]
        ctx_ps = ctx.enter_context(nc.psum_tensor("ctx_ps", [P, TOK], F32))
        upd_ps = ctx.enter_context(nc.psum_tensor("upd_ps", [P, TOK], F32))

        ident = cst[:, C_ID:C_ID + P]
        mask = cst[:, C_MASK:C_MASK + P]
        diag = cst[:, C_DIAG:C_DIAG + 2 * HW]

        in_fc, in_pr, in_qkv, in_wo, in_w1, in_w2, in_small, in_const = (
            sem(n) for n in ("in_fc", "in_pr", "in_qkv", "in_wo", "in_w1", "in_w2", "in_small", "in_const"))
        w1_split = sem("w1_split")
        stack_zero = sem("stack_zero")
        set_mem = sem("set_mem")
        set_act = sem("set_act")
        set_dve = sem("set_dve")
        set_pe = sem("set_pe")
        fb_done, fc_tern, u4_done, pr_tern, diag_done, g_lo_done = (
            sem(n) for n in ("fb_done", "fc_tern", "u4_done", "pr_tern", "diag_done", "g_lo_done"))
        PE_B, PE_FC, PE_G, PE_SC, PE_PR, PE_ALL = 1, 2, 6, 8, 9, 12
        ACT_SUMS, ACT_B, ACT_FC, ACT_G, ACT_SC, ACT_ALL = HB + KE, HB + KE + 1, HB + KE + 2, HB + KE + 6, HB + KE + 8, HB + KE + 12
        DVE_ALL = 30
        x_in = sem("x_in")
        tab_in = sem("tab_in")
        out_sent = sem("out_sent")
        ln_stats = sem("ln_stats")
        ln_pow = sem("ln_pow")
        xn_done = sem("xn_done")
        xb_done = sem("xb_done")
        xs_done = sem("xs_done")
        xnb_done = sem("xnb_done")
        shared_full = sem("shared_full")
        shared_free = sem("shared_free")
        xT_hi_done = sem("xT_hi_done")
        dense_full = sem("dense_full")
        dense_free = sem("dense_free")
        k_parts_done = sem("k_parts_done")
        q_parts_done = sem("q_parts_done")
        stack_in = sem("stack_in")
        v_trig_done = sem("v_trig_done")
        q_trig_done = sem("q_trig_done")
        upd_full = sem("upd_full")
        upd_free = sem("upd_free")
        z_hi_done = sem("z_hi_done")
        k_turned = sem("k_turned")
        k_tok_done = sem("k_tok_done")
        av_done = sem("av_done")
        ctx_full = sem("ctx_full")
        norm_done = sem("norm_done")
        ctx_free = sem("ctx_free")
        upd_used = sem("upd_used")
        wide_done = sem("wide_done")
        hi_done = sem("hi_done")
        lo_done = sem("lo_done")
        wide_used = sem("wide_used")
        cT_hi_done = sem("cT_hi_done")
        ssq_done = sem("ssq_done")
        r2_done = sem("r2_done")
        hs_done = sem("hs_done")
        res_done = sem("res_done")
        ffn_done = sem("ffn_done")
        out_done = sem("out_done")

        N_STATS = NB + 7
        N_SHARED = 26
        S_V, S_SCORE, S_CT, S_OUT, S_HT, S_XT = 0, 2, 18, 20, 22, 24
        MLP_BEFORE_KQ = 2
        N_DENSE = 2 * HB + 2 * KE

        def dense_use(t, n):
            return 2 * KE + t * N_DENSE + n

        def mlp_use(t, m, more):
            return dense_use(t, HB + m + (2 * KE if m >= MLP_BEFORE_KQ and more else 0))

        def kq_use(t, i):
            return dense_use(t, i - 2 * KE) if isinstance(t, int) and t == 0 else \
                dense_use(t - 1, HB + MLP_BEFORE_KQ + i)

        N_UPD = 1 + NB * KE

        def shared_use(t, n):
            return KE + t * N_SHARED + n

        def later(eng, sem_, n):
            if not isinstance(n, int) or n > 0:
                eng.wait_ge(sem_, n)

        def chunk_block(j):
            return (j % B) * 2 + j // B

        block = ctx.enter_context(nc.Block())

        @block.sync
        def _(sp):
            def load_x(t):
                for b in range(B):
                    sp.dma_start(xin[:, 2 * b:2 * b + 2, :],
                                 x[b, bass.ds(t * POS, POS), :].rearrange("(c p) e -> p c e", p=P)).then_inc(x_in, 16)

            def load_tab(t):
                sp.dma_start(tab[:, :], trig[bass.ds(t, 1), :, :].rearrange("a p n -> p (a n)")).then_inc(tab_in, 16)

            load_x(0)
            sp.dma_start(cst[:, :], consts).then_inc(in_const, 16)
            load_tab(0)
            sp.dma_start(raw_qkv, qkv_w.rearrange("(k p) n -> p k n", p=P)).then_inc(in_qkv, 16)
            sp.dma_start(raw_fc, w_fc.rearrange("(m p) n -> p m n", p=P)).then_inc(in_fc, 16)
            sp.dma_start(raw_pr, w_proj.rearrange("(m p) n -> p m n", p=P)).then_inc(in_pr, 16)
            sp.dma_start(raw_wo, out_w.rearrange("(k p) n -> p k n", p=P)).then_inc(in_wo, 16)
            sp.dma_start(raw_w1, mlp_w1.rearrange("(k p) n -> p k n", p=P)).then_inc(in_w1, 16)
            sp.wait_ge(w1_split, 1)
            sp.dma_start(raw_w2, mlp_w2.rearrange("(k p) n -> p k n", p=P)).then_inc(in_w2, 16)

            def stack(t):
                sp.wait_ge(k_parts_done, t * 2 + 2)
                if not isinstance(t, int) or t:
                    sp.wait_ge(shared_full, shared_use(t - 1, S_SCORE + 4 * NB))
                for parts, done, slots, which in ((k_parts, k_parts_done, (0, 0, 1), 0),
                                                  (q_parts, q_parts_done, (0, 1, 0), 1)):
                    sp.wait_ge(done, t * 2 + 2)
                    for g in range(4):
                        for s_, part in enumerate(slots):
                            if which == 0:
                                sp.dma_start(k_stack[s_:P:4, g, :, :].bitcast(F32),
                                             parts[32 * g:32 * g + 32, part, :, :]).then_inc(stack_in, 16)
                            else:
                                for r in range(2):
                                    sp.dma_start(q_stack[64 * r + s_:64 * r + 64:4, g, r, :, :].bitcast(F32),
                                                 parts[32 * g + 16 * r:32 * g + 16 * r + 16, part, :, :]
                                                 ).then_inc(stack_in, 16)

            sp.wait_ge(stack_zero, 2)
            stack(0)

            def body(t, more):
                if more:
                    sp.wait_ge(xn_done, (t + 1) * NB)
                    sp.wait_ge(xb_done, t + 1)
                    load_x(t + 1)
                    sp.wait_ge(q_trig_done, (t + 1) * 2 * NB)
                    sp.wait_ge(v_trig_done, (t + 1) * 2 * NB)
                    load_tab(t + 1)
                    stack(t + 1)
                for b in range(B):
                    sp.wait_ge(out_done, t * 2 + b + 1)
                    sp.dma_start(out[b, bass.ds(t * POS, POS), :].rearrange("(c p) e -> p c e", p=P),
                                 res[:, 2 * b:2 * b + 2, :]).then_inc(out_sent, 16)

            body(0, True)
            with sp.Fori(1, NT - 1) as t:
                body(t, True)
            body(NT - 1, False)
            sp.wait_ge(out_sent, NT * 32)

        @block.gpsimd
        def _(pool):
            pool.memset(half[:, :], -0.5).then_inc(set_mem, 1)
            pool.memset(rms_eps[:, :], RMS_EPS).then_inc(set_mem, 1)
            pool.memset(inv_e[:, :], 1.0 / E).then_inc(set_mem, 1)
            pool.memset(ones[:, :], 1.0).then_inc(set_mem, 1)
            pool.memset(state[:, :, :, :].rearrange("p b k n -> p (b k n)"), 0.0).then_inc(set_mem, 1)
            pool.memset(fb4.rearrange("p q r -> p (q r)"), 0.0).then_inc(set_mem, 1)
            pool.memset(u4.rearrange("p m q r -> p (m q r)"), 0.0).then_inc(set_mem, 1)

            def inverse_root(t):
                pool.wait_ge(ln_stats, t * N_STATS + N_STATS)
                pool.tensor_tensor(rstd[:, :], var_eps[:, :], half[:, :], ALU.pow).then_inc(ln_pow, 1)
                pool.wait_ge(ln_pow, t * 6 + 1)
                pool.tensor_tensor(rstd2[:, :], rstd[:, :], rstd[:, :], ALU.mult).then_inc(ln_pow, 1)
                pool.wait_ge(ln_pow, t * 6 + 2)
                pool.tensor_tensor(msq[:, :], rstd2[:, :], var[:, :], ALU.mult).then_inc(ln_pow, 1)
                pool.wait_ge(ln_pow, t * 6 + 3)
                pool.tensor_tensor(r1_sq_inv[:, :], msq[:, :], rms_eps[:, :], ALU.add).then_inc(ln_pow, 1)
                pool.wait_ge(ln_pow, t * 6 + 4)
                pool.tensor_tensor(r1[:, :], r1_sq_inv[:, :], half[:, :], ALU.pow).then_inc(ln_pow, 1)

            def keep_msq(t):
                pool.tensor_tensor(msq_eps[:, :], msq[:, :], rms_eps[:, :], ALU.add).then_inc(ln_pow, 1)

            def x_plus_b2(t):
                pool.tensor_tensor(xb[:, :, :], xin[:, :, :],
                                   b2_row[:, :].rearrange("p (a n) -> p a n", a=1).broadcast_to([P, NB, E]),
                                   ALU.add).then_inc(xb_done, 1)

            pool.wait_ge(set_mem, 7)
            inverse_root(0)
            keep_msq(0)
            pool.memset(k_stack[:, :, :, :].rearrange("p g m n -> p (g m n)").bitcast(F32), 0.0).then_inc(stack_zero, 1)
            pool.memset(q_stack[:, :, :, :, :].rearrange("p g r m n -> p (g r m n)").bitcast(F32), 0.0).then_inc(stack_zero, 1)
            pool.wait_ge(x_in, 32)
            pool.wait_ge(in_small, 16 * N_SMALL)
            pool.wait_ge(set_act, ACT_SUMS)
            x_plus_b2(0)

            def body(t, more):
                def trig_q(j):
                    k = chunk_block(j)
                    later(pool, ctx_full, t * NB + max(j - 1, 0))
                    for r in range(2):
                        cols = r * POS + (k % 2) * P
                        row = tab[:, cols:cols + P].rearrange("p (a n) -> p a n", a=1)
                        pool.tensor_tensor(q_trig[:, j % 2, r, :, :], qT[:, :, k * P:(k + 1) * P],
                                           row.broadcast_to([P, KE, P]), ALU.mult).then_inc(q_trig_done, 1)

                pool.wait_ge(tab_in, t * 16 + 16)
                pool.wait_ge(dense_free, kq_use(t, 3) + 1)
                pool.wait_ge(stack_in, (t + 1) * N_STACK * 16)
                trig_q(0)
                pool.wait_ge(xs_done, (t + 1) * NB)
                pool.wait_ge(xn_done, (t + 1) * NB)
                pool.tensor_tensor(xn[:, :, :], xn[:, :, :],
                                   ob_row[:, :].rearrange("p (a n) -> p a n", a=1).broadcast_to([P, NB, E]),
                                   ALU.add).then_inc(xnb_done, 1)

                for j in range(NB):
                    if j + 1 < NB:
                        trig_q(j + 1)
                    for m in range(KE):
                        n = j * KE + m
                        pool.wait_ge(upd_free, t * N_UPD + 2 + n)
                        pool.wait_ge(ctx_full, t * NB + j + 1)
                        later(pool, upd_used, t * NB * KE + max(n - 3, 0))
                        pool.tensor_tensor(state[:, j % B, m, :], state[:, j % B, m, :], added[:, n % 2, :],
                                           ALU.add).then_inc(upd_used, 1)
                if more:
                    inverse_root(t + 1)
                pool.wait_ge(ssq_done, (t + 1) * NB)
                pool.tensor_tensor(ms2[:, :], ssq[:, :], inv_e[:, :], ALU.mult).then_inc(r2_done, 1)
                pool.wait_ge(r2_done, t * 3 + 1)
                pool.tensor_tensor(ms2[:, :], ms2[:, :], rms_eps[:, :], ALU.add).then_inc(r2_done, 1)
                pool.wait_ge(r2_done, t * 3 + 2)
                pool.tensor_tensor(r2[:, :], ms2[:, :], half[:, :], ALU.pow).then_inc(r2_done, 1)
                pool.wait_ge(shared_free, shared_use(t, S_OUT + 1) + 1)
                later(pool, out_sent, t * 32)
                pool.tensor_tensor(res, xb[:, :, :], ctxn, ALU.add).then_inc(res_done, 1)
                pool.wait_ge(ffn_done, (t + 1) * NB)
                pool.wait_ge(res_done, t * 2 + 1)
                pool.tensor_tensor(res, res, ctxn, ALU.add).then_inc(res_done, 1)
                if more:
                    keep_msq(t + 1)
                    pool.wait_ge(x_in, t * 32 + 64)
                    x_plus_b2(t + 1)

            body(0, True)
            with pool.Fori(1, NT - 1) as t:
                body(t, True)
            body(NT - 1, False)

        @block.scalar
        def _(act):
            smalls = [
                (b2_row[:, :], mlp_b2.rearrange("(a n) -> a n", a=1).broadcast_to([P, E])),
                (n1w[:, :], norm1_w.rearrange("(k p) -> p k", p=P)),
                (n2w[:, :], norm2_w.rearrange("(k p) -> p k", p=P)),
                (qkb[:, :], qkv_b[0:2 * E].rearrange("(k p) -> p k", p=P)),
                (vb_row[:, :], qkv_b[2 * E:3 * E].rearrange("(a n) -> a n", a=1).broadcast_to([P, E])),
                (ob_row[:, :], out_b.rearrange("(a n) -> a n", a=1).broadcast_to([P, E])),
                (b1[:, :], mlp_b1.rearrange("(k p) -> p k", p=P)),
                (gate_col[:, :], gate.broadcast_to([P, 1])),
                (u_raw, u.rearrange("(m p) r -> p m r", p=P)),
                (v_raw, v),
                (fbT, fast_b.rearrange("r k -> k r")),
            ]
            assert len(smalls) == N_SMALL
            for dst, src in smalls:
                act.dma_start(dst, src, allow_slow_non_contiguous=True).then_inc(in_small, 16)

            n = 0
            for m in range(HB):
                if m == 0:
                    act.wait_ge(in_fc, 16)
                act.activation(junk[:, (m % 2) * E:(m % 2 + 1) * E], raw_fc[:, m, :], ACT.Abs, accum_out=sums[:, m:m + 1]).then_inc(set_act, 1)
                n += 1
                act.wait_ge(set_act, n)
            act.wait_ge(in_pr, 16)
            for m in range(KE):
                act.activation(junk, raw_pr[:, m, :], ACT.Abs, accum_out=sums[:, HB + m:HB + m + 1]).then_inc(set_act, 1)
                n += 1
                act.wait_ge(set_act, n)
            def scale_x(t):
                act.wait_ge(ln_pow, t * 6 + 5)
                for k in range(NB):
                    act.wait_ge(xn_done, t * NB + k + 1)
                    act.activation(xs[:, k, :], xn[:, k, :], ACT.Copy, scale=r1[:, k:k + 1]).then_inc(xs_done, 1)

            def x_hi(t):
                for m in range(KE):
                    act.wait_ge(shared_full, shared_use(t, m - KE) + 1)
                    act.activation(xT_hi[:, m, :], shared[m][:, :], ACT.Copy).then_inc(xT_hi_done, 1)

            def relu_kq(t):
                if not isinstance(t, int) or t:
                    act.wait_ge(q_trig_done, t * 2 * NB)
                for i, (dst, base) in enumerate(((kT, KE), (qT, 0))):
                    for m in range(KE):
                        act.wait_ge(dense_full, kq_use(t, i * KE + m) + 1)
                        act.activation(dst[:, m, :], dense[m][:, :], ACT.Relu,
                                       bias=qkb[:, base + m:base + m + 1]).then_inc(dense_free, 1)

            scale_x(0)
            x_hi(0)
            act.wait_ge(set_pe, PE_B)
            act.activation(zw_hi[:, :, :].rearrange("p k n -> p (k n)"), upd_ps[:, 0:KE * P], ACT.Copy).then_inc(set_act, 1)
            for m in range(KE):
                for g in range(2):
                    act.wait_ge(set_pe, PE_FC + m * 2 + g)
                    act.activation(fcT[:, m, g * TOK:(g + 1) * TOK], (dense + accum)[m * 2 + g][:, :],
                                   ACT.Copy).then_inc(set_act, 1)
            for g in range(2):
                act.wait_ge(set_pe, PE_G + g)
                act.activation(gT[:, g * TOK:(g + 1) * TOK], dense[g][:, :], ACT.Copy).then_inc(set_act, 1)
            act.wait_ge(set_pe, PE_SC)
            act.activation(pr_scale_row[:, :], ctx_ps[:, 0:E], ACT.Copy).then_inc(set_act, 1)
            for g in range(4):
                act.wait_ge(set_pe, PE_PR + g)
                act.activation(prT[:, 2 * g:2 * g + 2, :].rearrange("p h n -> p (h n)"),
                               (dense + accum)[g][:, :], ACT.Copy).then_inc(set_act, 1)
            act.wait_ge(set_dve, DVE_ALL)
            relu_kq(0)

            def body(t, more):
                act.wait_ge(upd_full, t * N_UPD + 1)
                act.activation(z_st[:, :], upd_ps[:, :], ACT.Copy).then_inc(z_hi_done, 1)
                for g in range(2):
                    act.wait_ge(k_turned, t * 2 + g + 1)
                    act.activation(k_tok[:, 2 * g:2 * g + 2, :].rearrange("p b n -> p (b n)"), accum[g][:, :],
                                   ACT.Copy).then_inc(k_tok_done, 1)

                def ffn_block(m):
                    act.wait_ge(dense_full, dense_use(t, m) + 1)
                    later(act, wide_used, t * 2 * HB + max(m - 1, 0))
                    act.activation(wide[:, m % 2, :], dense[m % 2][:, :], ACT.Relu,
                                   scale=scales[:, m:m + 1]).then_inc(dense_free, 1)
                    act.wait_ge(dense_free, dense_use(t, m) + 1)
                    act.activation(wide[:, m % 2, :], wide[:, m % 2, :], ACT.Square).then_inc(wide_done, 1)

                def mlp_block(m):
                    act.wait_ge(dense_full, mlp_use(t, m, more) + 1)
                    act.wait_ge(wide_used, t * 2 * HB + HB + m - 1)
                    act.activation(wide[:, m % 2, :], dense[m % 2][:, :], ACT.Gelu_apprx_tanh,
                                   bias=b1[:, m:m + 1]).then_inc(dense_free, 1)

                def trig_v(j):
                    k = chunk_block(j)
                    act.wait_ge(shared_free, shared_use(t, S_V + k // 2) + 1)
                    later(act, upd_full, t * N_UPD + max(2 * j - 1, 0))
                    for r in range(2):
                        c = 2 * POS + 2 * r + k % 2
                        act.activation(v_trig[:, j % 2, :, r, :],
                                       v_tok[:, k, :, :].rearrange("p (m h) e -> p m (h e)", m=KE),
                                       ACT.Copy, scale=tab[:, c:c + 1]).then_inc(v_trig_done, 1)

                ffn_block(0)
                ffn_block(1)
                act.wait_ge(tab_in, t * 16 + 16)
                act.wait_ge(stack_in, (t + 1) * N_STACK * 16)
                trig_v(0)
                for j in range(NB):
                    if j + 1 < NB:
                        trig_v(j + 1)
                    ffn_block(j + 2)
                for m in range(KE):
                    act.wait_ge(shared_full, shared_use(t, S_CT + m) + 1)
                    act.activation(cT_hi[:, m, :], shared[m][:, :], ACT.Copy).then_inc(cT_hi_done, 1)
                ffn_block(6)
                for k in range(NB):
                    act.wait_ge(shared_free, shared_use(t, S_OUT + k // 2) + 1)
                    act.activation(xs[:, k, :], ctxn[:, k, :], ACT.Square,
                                   accum_out=ssq[:, k:k + 1]).then_inc(ssq_done, 1)
                ffn_block(7)
                for m in range(KE):
                    act.wait_ge(shared_full, shared_use(t, S_HT + m) + 1)
                    act.activation(cT_hi[:, m, :], shared[m][:, :], ACT.Copy).then_inc(cT_hi_done, 1)
                if more:
                    scale_x(t + 1)
                for m in range(HB):
                    mlp_block(m)
                    if m == 0 and more:
                        x_hi(t + 1)
                    if m == MLP_BEFORE_KQ - 1 and more:
                        relu_kq(t + 1)

            body(0, True)
            with act.Fori(1, NT - 1) as t:
                body(t, True)
            body(NT - 1, False)

        @block.vector
        def _(dve):
            def ln_statistics(t):
                dve.wait_ge(x_in, t * 32 + 32)
                later(dve, ln_pow, t * 6)
                for k in range(NB):
                    dve.bn_stats(stats[:, k, :], xin[:, k, :]).then_inc(ln_stats, 1)

            def moments(t):
                base = t * N_STATS
                dve.wait_ge(ln_stats, base + NB)
                for dst, col, op in ((mean_sum, 1, ALU.add), (mean_dif, 1, ALU.subtract), (var_sum, 2, ALU.add)):
                    dve.tensor_tensor(dst[:, :], stats[:, :, col], stats[:, :, 3 + col], op).then_inc(ln_stats, 1)
                dve.wait_ge(ln_stats, base + NB + 3)
                dve.scalar_tensor_tensor(dif_sq[:, :], mean_dif[:, :], 0.25, mean_dif[:, :],
                                         ALU.mult, ALU.mult).then_inc(ln_stats, 1)
                dve.tensor_scalar(mean[:, :], mean_sum[:, :], 0.5, None, ALU.mult).then_inc(ln_stats, 1)
                dve.wait_ge(ln_stats, base + NB + 5)
                dve.scalar_tensor_tensor(var[:, :], var_sum[:, :], 1.0 / E, dif_sq[:, :],
                                         ALU.mult, ALU.add).then_inc(ln_stats, 1)
                dve.wait_ge(ln_stats, base + NB + 6)
                dve.tensor_scalar(var_eps[:, :], var[:, :], LN_EPS, None, ALU.add).then_inc(ln_stats, 1)

            def layernorm(t):
                dve.wait_ge(ln_pow, t * 6 + 1)
                for k in range(NB):
                    dve.tensor_scalar(xn[:, k, :], xin[:, k, :], mean[:, k:k + 1], rstd[:, k:k + 1],
                                      ALU.subtract, ALU.mult).then_inc(xn_done, 1)

            def x_lo(t):
                for m in range(KE):
                    dve.wait_ge(xT_hi_done, t * KE + m + 1)
                    dve.tensor_tensor(xT_lo[:, m, :], shared[m][:, :], xT_hi[:, m, :].bitcast(F32),
                                      ALU.subtract).then_inc(shared_free, 1)

            def split_weights(n, weights):
                for src, load, scale, hi, lo in weights:
                    dve.wait_ge(load, 16)
                    if scale is not None:
                        for k in range(KE):
                            dve.tensor_scalar(src[:, k, :], src[:, k, :], scale[:, k:k + 1], None, ALU.mult).then_inc(set_dve, 1)
                            n += 1
                        dve.wait_ge(set_dve, n)
                    dve.tensor_copy(hi[:, :, :], src).then_inc(set_dve, 1)
                    n += 1
                    dve.wait_ge(set_dve, n)
                    dve.tensor_tensor(lo[:, :, :], src, hi[:, :, :].bitcast(F32), ALU.subtract).then_inc(set_dve, 1)
                    n += 1
                    if src is raw_w1:
                        dve.wait_ge(set_dve, n)
                        dve.sem_inc(w1_split, 1)
                return n

            def kq_parts(t):
                if not isinstance(t, int) or t:
                    dve.wait_ge(av_done, t * 4 * NB)
                for src, parts, i, done in ((kT, k_parts, KE - 1, k_parts_done), (qT, q_parts, 2 * KE - 1, q_parts_done)):
                    dve.wait_ge(dense_free, kq_use(t, i) + 1)
                    dve.tensor_copy(parts[:, 0, :, :].bitcast(F32R), src).then_inc(done, 1)
                    dve.wait_ge(done, t * 2 + 1)
                    dve.tensor_tensor(parts[:, 1, :, :].bitcast(F32R), src, parts[:, 0, :, :],
                                      ALU.subtract).then_inc(done, 1)

            ln_statistics(0)
            moments(0)
            layernorm(0)
            dve.wait_ge(in_small, 16 * N_SMALL)
            dve.wait_ge(in_const, 16)
            dve.wait_ge(set_mem, 7)
            dve.tensor_copy(fb4[:, :, 0:RANK], fbT.rearrange("p (a r) -> p a r", a=1).broadcast_to([RANK, 4, RANK])
                            ).then_inc(fb_done, 1)
            n = 0
            n = split_weights(n, ((raw_qkv, in_qkv, n1w, wqkv_hi, wqkv_lo), (raw_w1, in_w1, n2w, w1_hi, w1_lo)))
            dve.wait_ge(set_act, ACT_SUMS)
            for lo_c, hi_c, count in ((0, HB, E), (HB, HB + KE, HID)):
                dve.tensor_scalar(scales[:, lo_c:hi_c], sums[:, lo_c:hi_c], 1.0 / count, 1e-5,
                                  ALU.mult, ALU.max).then_inc(set_dve, 1)
                n += 1
            dve.wait_ge(set_dve, n)
            dve.tensor_scalar(half_pos[:, :], scales[:, :], 0.5, None, ALU.mult).then_inc(set_dve, 1)
            dve.tensor_scalar(half_neg[:, :], scales[:, :], -0.5, None, ALU.mult).then_inc(set_dve, 1)
            dve.reciprocal(g_by_s[:, :], scales[:, 0:HB]).then_inc(set_dve, 1)
            n += 3
            for m in range(HB):
                dve.wait_ge(set_dve, n)
                dve.tensor_scalar(less[:, m % 2, 0:E], raw_fc[:, m, :], half_neg[:, m:m + 1], None,
                                  ALU.is_lt).then_inc(set_dve, 1)
                n += 1
                dve.wait_ge(set_dve, n)
                dve.scalar_tensor_tensor(raw_fc[:, m, :], raw_fc[:, m, :], half_pos[:, m:m + 1], less[:, m % 2, 0:E],
                                         ALU.is_gt, ALU.subtract).then_inc(fc_tern, 1)
            dve.tensor_scalar(g_by_s[:, :], g_by_s[:, :], gate_col[:, 0:1], None, ALU.mult).then_inc(set_dve, 1)
            n += 1
            dve.wait_ge(set_dve, n)
            for q in range(4):
                dve.tensor_tensor(u4[:, :, q, 0:RANK], u_raw,
                                  g_by_s[:, :].rearrange("p (m a) -> p m a", a=1).broadcast_to([P, HB, RANK]),
                                  ALU.mult).then_inc(u4_done, 1)
            dve.wait_ge(fc_tern, HB)
            for m in range(KE):
                both = less[:, :, :].rearrange("p a n -> p (a n)")
                c = HB + m
                dve.wait_ge(pr_tern, m)
                dve.tensor_scalar(both, raw_pr[:, m, :], half_neg[:, c:c + 1], None, ALU.is_lt).then_inc(set_dve, 1)
                n += 1
                dve.wait_ge(set_dve, n)
                dve.scalar_tensor_tensor(raw_pr[:, m, :], raw_pr[:, m, :], half_pos[:, c:c + 1], both,
                                         ALU.is_gt, ALU.subtract).then_inc(pr_tern, 1)
                dve.tensor_scalar(diag_scale[:, m, :], ident, scales[:, c:c + 1], None, ALU.mult).then_inc(diag_done, 1)
            x_lo(0)
            dve.wait_ge(set_act, ACT_B)
            dve.tensor_tensor(zw_lo[:, :, :].rearrange("p k n -> p (k n)"), upd_ps[:, 0:KE * P],
                              zw_hi[:, :, :].rearrange("p k n -> p (k n)").bitcast(F32), ALU.subtract).then_inc(set_dve, 1)
            n += 1
            for g in range(2):
                dve.wait_ge(set_act, ACT_G + g)
                for r in (32, 96):
                    part = gT[r:r + 32, g * TOK:(g + 1) * TOK]
                    dve.tensor_tensor(part, dense[g][r:r + 32, :], part.bitcast(F32), ALU.subtract).then_inc(g_lo_done, 1)
            n = split_weights(n, ((raw_wo, in_wo, None, wo_hi, wo_lo), (raw_w2, in_w2, None, w2_hi, w2_lo)))
            dve.wait_ge(set_dve, n)
            dve.wait_ge(set_pe, PE_ALL)
            dve.memset(v_tok[:, :, :, D:VW].rearrange("p b h e -> p (b h) e"), 1.0).then_inc(set_dve, 1)
            n += 1
            assert n == DVE_ALL, n
            kq_parts(0)

            def body(t, more):
                later(dve, v_trig_done, t * 2 * NB)
                for g in range(2):
                    dve.wait_ge(shared_full, shared_use(t, S_V + g) + 1)
                    for_block = shared[g][:, :].rearrange("p (b h e) -> p b h e", b=2, h=H)
                    bias = vb_row[:, :].rearrange("p (a h e) -> p a h e", a=1, h=H).broadcast_to([P, 2, H, D])
                    dve.tensor_tensor(v_tok[:, 2 * g:2 * g + 2, :, 0:D], for_block, bias, ALU.add).then_inc(shared_free, 1)
                dve.wait_ge(z_hi_done, t + 1)
                dve.tensor_tensor(z_st[64:128, :], upd_ps[64:128, :], z_st[64:128, :].bitcast(F32),
                                  ALU.subtract).then_inc(upd_free, 1)

                def split(n):
                    if n < HB:
                        dve.wait_ge(wide_done, t * HB + n + 1)
                    else:
                        dve.wait_ge(dense_free, mlp_use(t, n - HB, more) + 1)
                    dve.tensor_copy(wide_hi[:, n % 2, :], wide[:, n % 2, :]).then_inc(hi_done, 1)
                    dve.wait_ge(hi_done, t * 2 * HB + n + 1)
                    dve.tensor_tensor(wide_lo[:, n % 2, :], wide[:, n % 2, :], wide_hi[:, n % 2, :].bitcast(F32),
                                      ALU.subtract).then_inc(lo_done, 1)

                def weigh(j, g):
                    i = 4 * j + g
                    dve.wait_ge(shared_full, shared_use(t, S_SCORE + i) + 1)
                    later(dve, av_done, t * 4 * NB + max(i - 3, 0))
                    dve.tensor_tensor(weighted[:, g, :].rearrange("p (a n) -> p a n", a=4),
                                      shared[g % 2][:, :].rearrange("p (a n) -> p a n", a=4),
                                      mask.rearrange("p (a n) -> p a n", a=1).broadcast_to([P, 4, P]),
                                      ALU.mult).then_inc(shared_free, 1)

                def context(j):
                    heads = ctx_ps[:, 0:H * VW].rearrange("p (h e) -> p h e", e=VW)
                    c = t * 2 * NB + 2 * j
                    dve.wait_ge(ctx_full, t * NB + j + 1)
                    dve.tensor_scalar(norm[:, :], heads[:, :, D], NORM_EPS, None, ALU.add).then_inc(norm_done, 1)
                    dve.wait_ge(norm_done, c + 1)
                    dve.reciprocal(recip[:, :], norm[:, :]).then_inc(norm_done, 1)
                    dve.wait_ge(norm_done, c + 2)
                    if j == 0:
                        later(dve, res_done, t * 2)
                    dve.tensor_tensor(ctxn[:, chunk_block(j), :].rearrange("p (h e) -> p h e", e=D), heads[:, :, 0:D],
                                      recip[:, :].rearrange("p (h a) -> p h a", a=1).broadcast_to([P, H, D]),
                                      ALU.mult).then_inc(ctx_free, 1)

                def mask_update(j, m):
                    n = j * KE + m
                    dve.wait_ge(upd_full, t * N_UPD + 2 + n)
                    later(dve, upd_used, t * NB * KE + max(n - 1, 0))
                    dve.tensor_tensor(added[:, n % 2, :], upd_ps[:, 0:2 * HW], diag, ALU.mult).then_inc(upd_free, 1)

                split(0)
                dve.wait_ge(stack_in, (t + 1) * N_STACK * 16)
                weigh(0, 0)
                weigh(0, 1)
                for j in range(NB):
                    weigh(j, 2)
                    split(j + 1)
                    weigh(j, 3)
                    mask_update(j, 0)
                    context(j)
                    if j + 1 < NB:
                        weigh(j + 1, 0)
                        weigh(j + 1, 1)
                    mask_update(j, 1)
                    if j == 1 and more:
                        ln_statistics(t + 1)
                    if j == 2 and more:
                        moments(t + 1)
                for m in range(KE):
                    dve.wait_ge(cT_hi_done, t * 2 * KE + m + 1)
                    dve.tensor_tensor(cT_lo[:, m, :], shared[m][:, :], cT_hi[:, m, :].bitcast(F32),
                                      ALU.subtract).then_inc(shared_free, 1)
                split(5)
                dve.wait_ge(xnb_done, t + 1)
                for g in range(2):
                    dve.wait_ge(shared_full, shared_use(t, S_OUT + g) + 1)
                    dve.tensor_tensor(ctxn[:, 2 * g:2 * g + 2, :].rearrange("p b n -> p (b n)"), shared[g][:, :],
                                      xn[:, 2 * g:2 * g + 2, :].rearrange("p b n -> p (b n)"), ALU.add).then_inc(shared_free, 1)
                split(6)
                if more:
                    layernorm(t + 1)
                dve.wait_ge(r2_done, t * 3 + 3)
                for k in range(NB):
                    dve.tensor_scalar(xs[:, k, :], ctxn[:, k, :], r2[:, k:k + 1], None, ALU.mult).then_inc(hs_done, 1)
                split(7)
                for m in range(KE):
                    dve.wait_ge(cT_hi_done, t * 2 * KE + KE + m + 1)
                    dve.tensor_tensor(cT_lo[:, m, :], shared[m][:, :], cT_hi[:, m, :].bitcast(F32),
                                      ALU.subtract).then_inc(shared_free, 1)
                dve.wait_ge(wide_used, t * 2 * HB + HB)
                dve.wait_ge(res_done, t * 2 + 1)
                for k in range(NB):
                    dve.scalar_tensor_tensor(ctxn[:, k, :], accum[k // 2][:, (k % 2) * E:(k % 2 + 1) * E],
                                             msq_eps[:, k:k + 1], pr_scale_row[:, :],
                                             ALU.mult, ALU.mult).then_inc(ffn_done, 1)
                for m in range(HB):
                    split(HB + m)
                    if m == 0 and more:
                        x_lo(t + 1)
                    if m == MLP_BEFORE_KQ - 1 and more:
                        kq_parts(t + 1)
                dve.wait_ge(res_done, t * 2 + 2)
                dve.wait_ge(wide_used, (t + 1) * 2 * HB)
                for g in range(2):
                    dve.tensor_tensor(res[:, 2 * g:2 * g + 2, :].rearrange("p b n -> p (b n)"), accum[g][:, :],
                                      res[:, 2 * g:2 * g + 2, :].rearrange("p b n -> p (b n)"), ALU.add).then_inc(out_done, 1)

            body(0, True)
            with dve.Fori(1, NT - 1) as t:
                body(t, True)
            body(NT - 1, False)

        @block.tensor
        def _(pe):
            def turn_x(t):
                pe.wait_ge(xs_done, (t + 1) * NB)
                for m in range(KE):
                    use = shared_use(t, m - KE)
                    if not isinstance(t, int) or t:
                        pe.wait_ge(shared_free, use - 1)
                    for k in range(NB):
                        mm = pe.transpose(shared[m][:, k * P:(k + 1) * P], xs[:, k, m * P:(m + 1) * P], ident)
                    mm.then_inc(shared_full, 1)

            def dense_bank(use, n):
                later(pe, dense_free, use - 1)
                return dense[n % 2]

            def product3(dst, w_hi, w_lo, a_hi, a_lo, cols):
                for k in range(KE):
                    for i, (w, a) in enumerate(((w_hi, a_hi), (w_hi, a_lo), (w_lo, a_hi))):
                        mm = pe.matmul(dst, w[:, k, cols], a[:, k, :], start=(k == 0 and i == 0),
                                       stop=(k == KE - 1 and i == 2))
                return mm

            def make_kq(t):
                pe.wait_ge(shared_free, shared_use(t, -1) + 1)
                for i, base in enumerate((E, E + P, 0, P)):
                    bank = dense_bank(kq_use(t, i), i)
                    product3(bank[:, :], wqkv_hi, wqkv_lo, xT_hi, xT_lo,
                             slice(base, base + P)).then_inc(dense_full, 1)

            pe.wait_ge(in_const, 16)
            turn_x(0)
            pe.wait_ge(fb_done, 1)
            for m in range(KE):
                mm = pe.matmul(upd_ps[:, m * P:(m + 1) * P], v_raw[:, m * P:(m + 1) * P],
                               fb4.rearrange("p q r -> p (q r)"), start=True, stop=True)
            mm.then_inc(set_pe, 1)
            pe.wait_ge(fc_tern, HB)
            for m in range(KE):
                for g in range(2):
                    for i in range(4):
                        mm = pe.transpose((dense + accum)[m * 2 + g][:, i * P:(i + 1) * P],
                                          raw_fc[:, 4 * g + i, m * P:(m + 1) * P], ident)
                    mm.then_inc(set_pe, 1)
            pe.wait_ge(u4_done, 4)
            pe.wait_ge(set_act, ACT_FC + 1)
            for g in range(2):
                for i in range(4):
                    mm = pe.transpose(dense[g][:, i * P:(i + 1) * P],
                                      u4[:, 4 * g + i, :, :].rearrange("p q r -> p (q r)"), ident)
                mm.then_inc(set_pe, 1)
            pe.wait_ge(diag_done, KE)
            pe.matmul(ctx_ps[:, 0:E], ones[:, :], diag_scale.rearrange("p k n -> p (k n)"),
                      start=True, stop=True).then_inc(set_pe, 1)
            pe.wait_ge(pr_tern, KE)
            pe.wait_ge(g_lo_done, 4)
            pe.wait_ge(set_act, ACT_G + 1)
            for g in range(4):
                for hb in range(2):
                    for m in range(KE):
                        mm = pe.transpose((dense + accum)[g][:, hb * E + m * P:hb * E + (m + 1) * P],
                                          raw_pr[:, m, (2 * g + hb) * P:(2 * g + hb + 1) * P], ident)
                mm.then_inc(set_pe, 1)
            pe.wait_ge(set_act, ACT_ALL)
            pe.wait_ge(set_dve, DVE_ALL)
            make_kq(0)

            def body(t, more):
                def shared_bank(n):
                    pe.wait_ge(shared_free, shared_use(t, n) - 1)
                    return shared[n % 2]

                for g in range(2):
                    bank = shared_bank(S_V + g)
                    for i in range(2):
                        tok = slice((2 * g + i) * P, (2 * g + i + 1) * P)
                        for k in range(KE):
                            for c, (a, w) in enumerate(((xT_hi, wqkv_hi), (xT_hi, wqkv_lo), (xT_lo, wqkv_hi))):
                                mm = pe.matmul(bank[:, i * E:(i + 1) * E], a[:, k, tok], w[:, k, 2 * E:3 * E],
                                               start=(k == 0 and c == 0), stop=(k == KE - 1 and c == 2))
                    mm.then_inc(shared_full, 1)
                later(pe, upd_free, t * N_UPD)
                product3(upd_ps[:, :], zw_hi, zw_lo, xT_hi, xT_lo, slice(0, P)).then_inc(upd_full, 1)
                later(pe, out_done, t * 2)
                pe.wait_ge(dense_free, kq_use(t, KE - 1) + 1)
                for g in range(2):
                    for i in range(2):
                        for m in range(KE):
                            mm = pe.transpose(accum[g][:, i * E + m * P:i * E + (m + 1) * P],
                                              kT[:, m, (2 * g + i) * P:(2 * g + i + 1) * P], ident)
                    mm.then_inc(k_turned, 1)

                def ffn_up(m, part):
                    bank = dense[m % 2]
                    if part == 0:
                        dense_bank(dense_use(t, m), m)
                    cols = slice(m * P, (m + 1) * P)
                    for i, a in enumerate((xT_hi, xT_lo)):
                        pe.matmul(bank[:, :], fcT[:, part, cols], a[:, part, :], start=(part == 0 and i == 0), stop=False)
                    if part:
                        if m == 0:
                            pe.wait_ge(upd_free, t * N_UPD + 1)
                        pe.matmul(bank[:, :], gT[:, cols], z_st[:, :], start=False, stop=True).then_inc(dense_full, 1)

                def down(n, pairs, halves):
                    first, last = n % HB == 0, n % HB == HB - 1
                    pe.wait_ge(lo_done, t * 2 * HB + n + 1)
                    for g in halves:
                        for k in (2 * g, 2 * g + 1):
                            tok = slice(k * P, (k + 1) * P)
                            for i, (a, w) in enumerate(pairs):
                                mm = pe.matmul(accum[g][:, (k % 2) * E:(k % 2 + 1) * E], a[:, n % 2, tok],
                                               w[:, n % HB, :], start=(first and i == 0 and k % 2 == 0),
                                               stop=(last and i == len(pairs) - 1), skip_group_check=True)
                    if halves[-1] == 1:
                        mm.then_inc(wide_used, 1)

                def ffn_down(m, halves=(0, 1)):
                    if m == 0 and halves[0] == 0:
                        pe.wait_ge(k_tok_done, t * 2 + 2)
                    down(m, ((wide_hi, prT), (wide_lo, prT)), halves)

                def scores(j, g):
                    bank = shared_bank(S_SCORE + 4 * j + g)
                    tok = slice(chunk_block(j) * P, (chunk_block(j) + 1) * P)
                    if j == 0 and g == 0:
                        pe.wait_ge(stack_in, (t + 1) * N_STACK * 16)
                    for i in range(2):
                        row, m = (2 * g + i) % 4, (2 * g + i) // 4
                        mm = pe.matmul(bank[:, i * 2 * P:(i + 1) * 2 * P].rearrange("p (r n) -> p r n", r=2),
                                       k_stack[:, row, m, tok], q_stack[:, row, :, m, tok], start=True, stop=True)
                    mm.then_inc(shared_full, 1)

                def within(j, g):
                    k = chunk_block(j)
                    if g == 0:
                        later(pe, ctx_free, t * NB + j)
                    pe.wait_ge(shared_free, shared_use(t, S_SCORE + 4 * j + g) + 1)
                    for i in range(4):
                        h = 4 * g + i
                        mm = pe.matmul(ctx_ps[:, h * VW:(h + 1) * VW], weighted[:, g, i * P:(i + 1) * P],
                                       v_tok[:, k, h, :], start=(g == 0 and i == 0), stop=False,
                                       skip_group_check=True)
                    mm.then_inc(av_done, 1)

                def across(j):
                    k = chunk_block(j)
                    pe.wait_ge(q_trig_done, t * 2 * NB + 2 * (j + 1))
                    later(pe, upd_used, t * NB * KE + max(j - 1, 0) * KE)
                    for m in range(KE):
                        for r in range(2):
                            mm = pe.matmul(ctx_ps[:, m * HW:(m + 1) * HW], q_trig[:, j % 2, r, m, :],
                                           state[:, j % B, m, r * HW:(r + 1) * HW], start=False,
                                           stop=(m == KE - 1 and r == 1), skip_group_check=True)
                    mm.then_inc(ctx_full, 1)

                def update(j, m):
                    k = chunk_block(j)
                    pe.wait_ge(upd_free, t * N_UPD + 1 + j * KE + m)
                    if j == 0:
                        pe.wait_ge(k_tok_done, t * 2 + 2)
                    pe.wait_ge(v_trig_done, t * 2 * NB + 2 * (j + 1))
                    pe.matmul(upd_ps[:, 0:2 * HW], k_tok[:, k, m * P:(m + 1) * P],
                              v_trig[:, j % 2, m, :, :].rearrange("p r n -> p (r n)"),
                              start=True, stop=True).then_inc(upd_full, 1)

                for m in range(2):
                    ffn_up(m, 0)
                    ffn_up(m, 1)
                scores(0, 0)
                scores(0, 1)
                for j in range(NB):
                    ffn_down(j, (0,))
                    scores(j, 2)
                    within(j, 0)
                    ffn_up(j + 2, 0)
                    scores(j, 3)
                    within(j, 1)
                    ffn_down(j, (1,))
                    within(j, 2)
                    update(j, 0)
                    within(j, 3)
                    ffn_up(j + 2, 1)
                    across(j)
                    if j + 1 < NB:
                        scores(j + 1, 0)
                        scores(j + 1, 1)
                    update(j, 1)
                pe.wait_ge(ctx_free, t * NB + NB)
                for m in range(KE):
                    bank = shared_bank(S_CT + m)
                    for k in range(NB):
                        mm = pe.transpose(bank[:, k * P:(k + 1) * P], ctxn[:, k, m * P:(m + 1) * P], ident)
                    mm.then_inc(shared_full, 1)
                ffn_down(4)
                ffn_up(6, 0)
                ffn_up(6, 1)
                pe.wait_ge(shared_free, shared_use(t, S_CT + 1) + 1)
                for g in range(2):
                    bank = shared_bank(S_OUT + g)
                    for i in range(2):
                        tok = slice((2 * g + i) * P, (2 * g + i + 1) * P)
                        for k in range(KE):
                            for c, (a, w) in enumerate(((cT_hi, wo_hi), (cT_hi, wo_lo), (cT_lo, wo_hi))):
                                mm = pe.matmul(bank[:, i * E:(i + 1) * E], a[:, k, tok], w[:, k, :],
                                               start=(k == 0 and c == 0), stop=(k == KE - 1 and c == 2))
                    mm.then_inc(shared_full, 1)
                ffn_down(5)
                ffn_up(7, 0)
                ffn_up(7, 1)
                ffn_down(6)
                pe.wait_ge(hs_done, (t + 1) * NB)
                for m in range(KE):
                    bank = shared_bank(S_HT + m)
                    for k in range(NB):
                        mm = pe.transpose(bank[:, k * P:(k + 1) * P], xs[:, k, m * P:(m + 1) * P], ident)
                    mm.then_inc(shared_full, 1)
                ffn_down(7)

                def mlp_up(m):
                    bank = dense_bank(mlp_use(t, m, more), m)
                    if m == 0:
                        pe.wait_ge(shared_free, shared_use(t, S_HT + 1) + 1)
                    product3(bank[:, :], w1_hi, w1_lo, cT_hi, cT_lo, slice(m * P, (m + 1) * P)).then_inc(dense_full, 1)

                def mlp_down(m):
                    if m == 0:
                        pe.wait_ge(ffn_done, (t + 1) * NB)
                    down(HB + m, ((wide_hi, w2_hi), (wide_hi, w2_lo), (wide_lo, w2_hi)), (0, 1))

                mlp_up(0)
                if more:
                    turn_x(t + 1)
                for m in range(1, HB):
                    mlp_up(m)
                    mlp_down(m - 1)
                    if m == MLP_BEFORE_KQ - 1 and more:
                        make_kq(t + 1)
                mlp_down(HB - 1)

            body(0, True)
            with pe.Fori(1, NT - 1) as t:
                body(t, True)
            body(NT - 1, False)


_INS = ["x", "qkv_w", "qkv_b", "out_w", "out_b", "norm1_w", "norm2_w", "mlp_w1", "mlp_b1", "mlp_w2", "mlp_b2"]
_FFN_INS = ["fast_b", "w_fc", "w_proj", "u", "v", "gate"]


def kernel(**inputs):
    import concourse.bacc as bacc
    from concourse.bass_utils import run_bass_kernel_spmd

    nc = bacc.Bacc("TRN2", target_bir_lowering=False, num_devices=1, dynamic_dma_scratch_size=1024)
    arrays, args = {}, []
    for name in ["L0_attn_" + n for n in _INS] + ["L0_ffn_" + n for n in _FFN_INS]:
        a = np.ascontiguousarray(inputs[name])
        if a.ndim == 0:
            a = a.reshape(1, 1)
        arrays[name] = a
        args.append(nc.dram_tensor(name, a.shape, mybir.dt.from_np(a.dtype), kind="ExternalInput").ap())
    for name, a in zip(("consts", "trig"), constants()):
        arrays[name] = a
        args.append(nc.dram_tensor(name, a.shape, F32, kind="ExternalInput").ap())
    args.append(nc.dram_tensor("out", (B, L, E), F32, kind="ExternalOutput").ap())
    program(nc, *args)
    r = run_bass_kernel_spmd(nc, [arrays], core_ids=[0])
    return r.results[0]["out"]
```

```python
from contextlib import ExitStack

import numpy as np

import concourse.bass as bass
from concourse import mybir

F32 = mybir.dt.float32
F32R = mybir.dt.float32r
ALU = mybir.AluOpType
ACT = mybir.ActivationFunctionType
AX_X = mybir.AxisListType.X

P = 128
B, L, E = 2, 2048, 256
H, D = 16, 16
NB = 4
TOK = NB * P
POS = TOK // B
NT = L // POS
KE = E // P
HID = 4 * E
HB = HID // P
VW = D + 1
HW = H // KE * VW
RANK = 16
LN_EPS, RMS_EPS, NORM_EPS = 1e-5, 1e-6, 1e-6

PAIRS = H // 2
PARTS = 3
N_K_STACK = 4 * PARTS
N_Q_STACK = 2 * PARTS * 2
N_SMALL = 8

C_ID, C_MASK, C_DIAG = 0, P, 2 * P
C_ALL = C_DIAG + 2 * HW


def constants():
    i = np.arange(P)
    c = np.zeros((P, C_ALL), np.float32)
    c[:, C_ID:C_ID + P] = np.eye(P)
    step = i[None, :] - i[:, None]
    c[:, C_MASK:C_MASK + P] = np.where(step >= 0, np.cos(np.pi / 2 * step / L), 0)
    own = np.repeat((i[:, None] // D == np.arange(H // KE)[None, :]), VW, 1)
    c[:, C_DIAG:C_DIAG + 2 * HW] = np.concatenate([own, own], 1)
    t = np.zeros((NT, P, 2 * POS + 4), np.float32)
    for n in range(NT):
        a = np.pi / 2 * (n * POS + np.arange(POS)) / L
        t[n, :, 0:POS] = np.cos(a)
        t[n, :, POS:2 * POS] = np.sin(a)
        for k in range(2):
            t[n, :, 2 * POS + k] = np.cos(a[k * P:(k + 1) * P])
            t[n, :, 2 * POS + 2 + k] = np.sin(a[k * P:(k + 1) * P])
    return c, t


def program(nc, x, qkv_w, qkv_b, out_w, out_b, norm1_w, norm2_w, mlp_w1, mlp_b1, mlp_w2, mlp_b2,
            fast_b, w_fc, w_proj, u, v, gate, consts, trig, out):
    with ExitStack() as ctx:
        def sb(name, shape, dt=F32):
            return ctx.enter_context(nc.sbuf_tensor(name, shape, dt))

        def sem(name):
            return ctx.enter_context(nc.semaphore(name))

        wqkv_hi, wqkv_lo = (sb(f"wqkv_{n}", [P, KE, 3 * E], F32R) for n in ("hi", "lo"))
        wo_hi, wo_lo = (sb(f"wo_{n}", [P, KE, E], F32R) for n in ("hi", "lo"))
        w1_hi, w1_lo = (sb(f"w1_{n}", [P, KE, HID], F32R) for n in ("hi", "lo"))
        w2_hi, w2_lo = (sb(f"w2_{n}", [P, HB, E], F32R) for n in ("hi", "lo"))
        fcT = sb("fcT", [P, KE, HID], F32R)
        prT = sb("prT", [P, HB, E], F32R)
        zw = sb("zw", [P, KE, P], F32R)
        gT = sb("gT", [P, HID], F32R)
        pr_scale_row = sb("pr_scale_row", [P, E])
        cst = sb("cst", [P, C_ALL])
        ones = sb("ones", [P, P])
        n1w = sb("n1w", [P, KE])
        n2w = sb("n2w", [P, KE])
        qkb = sb("qkb", [P, 2 * KE])
        vb_row = sb("vb_row", [P, E])
        ob_row = sb("ob_row", [P, E])
        b2_row = sb("b2_row", [P, E])
        b1 = sb("b1", [P, HB])
        gate_col = sb("gate_col", [P, 1])
        half = sb("half", [P, NB])

        xin = sb("xin", [P, NB, E])
        tab = sb("tab", [P, 2 * POS + 4])
        xn = sb("xn", [P, NB, E])
        xs = sb("xs", [P, NB, E])
        xb = sb("xb", [P, NB, E])
        late = sb("late", [P, 2, NB, E])
        res = late[:, 0, :, :]
        ctxn = late[:, 1, :, :]
        xT_hi, xT_lo = (sb(f"xT_{n}", [P, KE, TOK], F32R) for n in ("hi", "lo"))
        cT_hi, cT_lo = (sb(f"cT_{n}", [P, KE, TOK], F32R) for n in ("hi", "lo"))
        z_st = sb("z_st", [P, TOK], F32R)
        wide = sb("wide", [P, 2, TOK])
        wide_hi, wide_lo = (sb(f"wide_{n}", [P, 2, TOK], F32R) for n in ("hi", "lo"))
        k_stack = sb("k_stack", [P, 4, KE, TOK], F32R)
        q_stack = sb("q_stack", [P, 4, 2, KE, TOK], F32R)
        arena_words = 6272
        arena = sb("arena", [P, arena_words])
        weighted = sb("weighted", [P, 4, 4 * P])
        at = [0, 0]

        def carve(n, which=0):
            at[which] += n
            assert at[which] <= arena_words
            return arena[:, at[which] - n:at[which]]

        qT = carve(KE * TOK).rearrange("p (m n) -> p m n", m=KE)
        kT = carve(KE * TOK).rearrange("p (m n) -> p m n", m=KE)
        k_tok = carve(NB * E).rearrange("p (b n) -> p b n", b=NB)
        v_tok = carve(NB * H * VW).rearrange("p (b h e) -> p b h e", b=NB, h=H)
        ring = carve(2 * KE * 2 * P + 2 * KE * 2 * HW)
        q_trig = ring[:, 0:2 * KE * 2 * P].rearrange("p (s r m n) -> p s r m n", s=2, r=2, m=KE)
        v_trig = ring[:, 2 * KE * 2 * P:].rearrange("p (s m r n) -> p s m r n", s=2, m=KE, r=2)
        k_parts = weighted[:, :, :].rearrange("p g n -> p (g n)").rearrange("p (i m n) -> p i m n", i=2, m=KE)
        q_parts = ring[:, 0:2 * KE * TOK].rearrange("p (i m n) -> p i m n", i=2, m=KE)

        at[1] = 2 * KE * TOK
        raw_fc = carve(HB * E, 1).rearrange("p (m n) -> p m n", m=HB)
        at[1] = arena_words - (2 * KE * 2 * P + 2 * KE * 2 * HW)
        raw_qkv = carve(KE * 3 * E, 1).rearrange("p (k n) -> p k n", k=KE)
        raw_wo = carve(KE * E, 1).rearrange("p (k n) -> p k n", k=KE)
        raw_late = late[:, :, :, :].rearrange("p a b n -> p (a b n)")
        raw_pr = raw_late.rearrange("p (m n) -> p m n", m=KE)
        raw_w2 = raw_late.rearrange("p (k n) -> p k n", k=HB)
        raw_w1 = [t_[:, :, :].rearrange("p b n -> p (b n)") for t_ in (xs, xb)]
        less = wide[:, :, :]
        added = sb("added", [P, 2, 2 * HW])
        added_flat = added[:, :, :].rearrange("p a n -> p (a n)")
        v_raw = added_flat[0:RANK, 0:E]
        fbT = added_flat[0:RANK, E:E + RANK]
        fb4 = added_flat[0:RANK, E + RANK:E + RANK + P].rearrange("p (q r) -> p q r", q=4)
        u_raw = added_flat[:, E + RANK + P:E + RANK + P + HB * RANK].rearrange("p (m r) -> p m r", m=HB)
        diag_scale = added_flat[:, 0:E].rearrange("p (k n) -> p k n", k=KE)
        u4 = xb[:, :, :].rearrange("p b n -> p (b n)").rearrange("p (m q r) -> p m q r", m=HB, q=4)
        junk = wide[:, :, :].rearrange("p a n -> p (a n)")
        sums = sb("sums", [P, HB + KE])
        scales = sb("scales", [P, HB + KE])
        half_pos = sb("half_pos", [P, HB + KE])
        half_neg = sb("half_neg", [P, HB + KE])
        g_by_s = sb("g_by_s", [P, HB])
        state = sb("state", [P, B, KE, 2 * HW])
        norm = sb("norm", [P, H])
        recip = sb("recip", [P, H])
        stats = sb("stats", [P, NB, 6])
        mean_sum, mean_dif, var_sum, dif_sq, mean, var = (
            sb(n, [P, NB]) for n in ("mean_sum", "mean_dif", "var_sum", "dif_sq", "mean", "var"))
        var_eps = sb("var_eps", [P, NB])
        rstd = sb("rstd", [P, NB])
        rstd2 = sb("rstd2", [P, NB])
        msq = sb("msq", [P, NB])
        r1_sq_inv = sb("r1_sq_inv", [P, NB])
        msq_eps = sb("msq_eps", [P, NB])
        rms_eps = sb("rms_eps", [P, NB])
        r1 = sb("r1", [P, NB])
        mean_sq = sb("mean_sq", [P, NB])
        ms2 = sb("ms2", [P, NB])
        r2 = sb("r2", [P, NB])

        dense = [ctx.enter_context(nc.psum_tensor(f"dense{i}", [P, TOK], F32)) for i in range(2)]
        shared = [ctx.enter_context(nc.psum_tensor(f"shared{i}", [P, TOK], F32)) for i in range(2)]
        accum = [ctx.enter_context(nc.psum_tensor(f"accum{i}", [P, TOK], F32)) for i in range(2)]
        ctx_ps = ctx.enter_context(nc.psum_tensor("ctx_ps", [P, TOK], F32))
        upd_ps = ctx.enter_context(nc.psum_tensor("upd_ps", [P, TOK], F32))

        ident = cst[:, C_ID:C_ID + P]
        mask = cst[:, C_MASK:C_MASK + P]
        diag = cst[:, C_DIAG:C_DIAG + 2 * HW]

        in_fc, in_pr, in_qkv, in_wo, in_w2, in_n1, in_fb, in_small, in_const = (
            sem(n) for n in ("in_fc", "in_pr", "in_qkv", "in_wo", "in_w2", "in_n1", "in_fb", "in_small",
                             "in_const"))
        in_w1 = [sem(f"in_w1_{k}") for k in range(KE)]
        stack_zero = sem("stack_zero")
        set_mem = sem("set_mem")
        sums_done = sem("sums_done")
        zw_done = sem("zw_done")
        read_out = sem("read_out")
        w1_hi_done = sem("w1_hi_done")
        w1_lo_done = sem("w1_lo_done")
        qkv_split, wo_split, w2_split = (sem(n) for n in ("qkv_split", "wo_split", "w2_split"))
        set_dve = sem("set_dve")
        set_pe = sem("set_pe")
        ones_done = sem("ones_done")
        fb_done, zw_full, fc_tern, u4_done, pr_tern, diag_done, g_lo_done = (
            sem(n) for n in ("fb_done", "zw_full", "fc_tern", "u4_done", "pr_tern", "diag_done", "g_lo_done"))
        SET_FC, SET_G, SET_SC, SET_PR, SET_ALL = 0, 4, 6, 7, 11
        x_in = sem("x_in")
        tab_in = sem("tab_in")
        out_sent = sem("out_sent")
        ln_stats = sem("ln_stats")
        ln_pow = sem("ln_pow")
        xn_done = sem("xn_done")
        xb_done = sem("xb_done")
        xs_done = sem("xs_done")
        xnb_done = sem("xnb_done")
        shared_full = sem("shared_full")
        shared_free = sem("shared_free")
        xT_hi_done = sem("xT_hi_done")
        dense_full = sem("dense_full")
        dense_free = sem("dense_free")
        k_parts_done = sem("k_parts_done")
        q_parts_done = sem("q_parts_done")
        k_stacked = sem("k_stacked")
        q_stacked = [sem(f"q_stacked{i}") for i in range(2)]
        v_trig_done = sem("v_trig_done")
        q_trig_done = sem("q_trig_done")
        upd_full = sem("upd_full")
        upd_free = sem("upd_free")
        z_hi_done = sem("z_hi_done")
        k_turned = sem("k_turned")
        k_tok_done = sem("k_tok_done")
        av_done = sem("av_done")
        across_done = sem("across_done")
        norm_done = sem("norm_done")
        ctx_free = sem("ctx_free")
        upd_used = sem("upd_used")
        wide_done = sem("wide_done")
        hi_done = sem("hi_done")
        lo_done = sem("lo_done")
        wide_used = sem("wide_used")
        cT_hi_done = sem("cT_hi_done")
        ssq_done = sem("ssq_done")
        r2_done = sem("r2_done")
        hs_done = sem("hs_done")
        res_done = sem("res_done")
        ffn_done = sem("ffn_done")
        out_done = sem("out_done")

        N_STATS = NB + 7
        N_SHARED = 26
        S_V, S_SCORE, S_CT, S_OUT, S_HT, S_XT = 0, 2, 18, 20, 22, 24
        MLP_BEFORE_KQ = 2
        N_DENSE = 2 * HB + 2 * KE

        def dense_use(t, n):
            return 2 * KE + t * N_DENSE + n

        def mlp_use(t, m, more):
            return dense_use(t, HB + m + (2 * KE if m >= MLP_BEFORE_KQ and more else 0))

        def kq_use(t, i):
            return dense_use(t, i - 2 * KE) if isinstance(t, int) and t == 0 else \
                dense_use(t - 1, HB + MLP_BEFORE_KQ + i)

        N_UPD = 1 + NB * KE

        def shared_use(t, n):
            return KE + t * N_SHARED + n

        def later(eng, sem_, n):
            if not isinstance(n, int) or n > 0:
                eng.wait_ge(sem_, n)

        def chunk_block(j):
            return (j % B) * 2 + j // B

        block = ctx.enter_context(nc.Block())

        @block.sync
        def _(sp):
            def load_x(t):
                for b in range(B):
                    sp.dma_start(xin[:, 2 * b:2 * b + 2, :],
                                 x[b, bass.ds(t * POS, POS), :].rearrange("(c p) e -> p c e", p=P)).then_inc(x_in, 16)

            def load_tab(t):
                sp.dma_start(tab[:, :], trig[bass.ds(t, 1), :, :].rearrange("a p n -> p (a n)")).then_inc(tab_in, 16)

            load_x(0)
            sp.dma_start(n1w[:, :], norm1_w.rearrange("(k p) -> p k", p=P),
                         allow_slow_non_contiguous=True).then_inc(in_n1, 16)
            sp.dma_start(raw_qkv, qkv_w.rearrange("(k p) n -> p k n", p=P)).then_inc(in_qkv, 16)
            sp.dma_start(cst[:, :], consts).then_inc(in_const, 16)
            sp.dma_start(raw_fc, w_fc.rearrange("(m p) n -> p m n", p=P)).then_inc(in_fc, 16)
            sp.dma_start(raw_wo, out_w.rearrange("(k p) n -> p k n", p=P)).then_inc(in_wo, 16)
            sp.dma_start(raw_pr, w_proj.rearrange("(m p) n -> p m n", p=P)).then_inc(in_pr, 16)
            load_tab(0)
            sp.wait_ge(shared_full, KE)
            sp.dma_start(raw_w1[0], mlp_w1[0:P, :]).then_inc(in_w1[0], 16)

            def stack(t):
                sp.wait_ge(k_parts_done, (t + 1) * 2 * KE)
                if not isinstance(t, int) or t:
                    sp.wait_ge(shared_full, shared_use(t - 1, S_SCORE + 4 * NB))
                for g in range(4):
                    for slot, part in enumerate((0, 0, 1)):
                        sp.dma_start(k_stack[slot:P:4, g, :, :].bitcast(F32),
                                     k_parts[32 * g:32 * g + 32, part, :, :]).then_inc(k_stacked, 16)
                sp.wait_ge(q_parts_done, (t + 1) * 2 * KE)
                for g in range(4):
                    for slot, part in enumerate((0, 1, 0)):
                        for r in range(2):
                            row = 32 * g + 16 * r
                            sp.dma_start(q_stack[64 * r + slot:64 * r + 64:4, g, r, :, :].bitcast(F32),
                                         q_parts[row:row + 16, part, :, :]).then_inc(q_stacked[g // 2], 16)

            sp.wait_ge(stack_zero, 2)
            stack(0)

            def body(t, more):
                if more:
                    sp.wait_ge(xn_done, (t + 1) * NB)
                    sp.wait_ge(xb_done, t + 1)
                    load_x(t + 1)
                    sp.wait_ge(q_trig_done, (t + 1) * 2 * NB)
                    sp.wait_ge(v_trig_done, (t + 1) * 2 * NB)
                    load_tab(t + 1)
                    stack(t + 1)
                for b in range(B):
                    sp.wait_ge(out_done, t * 2 + b + 1)
                    sp.dma_start(out[b, bass.ds(t * POS, POS), :].rearrange("(c p) e -> p c e", p=P),
                                 res[:, 2 * b:2 * b + 2, :]).then_inc(out_sent, 16)

            body(0, True)
            with sp.Fori(1, NT - 1) as t:
                body(t, True)
            body(NT - 1, False)
            sp.wait_ge(out_sent, NT * 32)

        @block.gpsimd
        def _(pool):
            pool.memset(half[:, :], -0.5).then_inc(set_mem, 1)
            pool.memset(rms_eps[:, :], RMS_EPS).then_inc(set_mem, 1)
            pool.memset(ones[:, :], 1.0).then_inc(set_mem, 1)
            pool.memset(state[:, :, :, :].rearrange("p b k n -> p (b k n)"), 0.0).then_inc(set_mem, 1)
            pool.memset(fb4.rearrange("p q r -> p (q r)"), 0.0).then_inc(set_mem, 1)
            pool.memset(u4.rearrange("p m q r -> p (m q r)"), 0.0).then_inc(set_mem, 1)

            def inverse_root(t):
                pool.wait_ge(ln_stats, t * N_STATS + N_STATS)
                pool.tensor_tensor(rstd[:, :], var_eps[:, :], half[:, :], ALU.pow).then_inc(ln_pow, 1)
                pool.wait_ge(ln_pow, t * 6 + 1)
                pool.tensor_tensor(rstd2[:, :], rstd[:, :], rstd[:, :], ALU.mult).then_inc(ln_pow, 1)
                pool.wait_ge(ln_pow, t * 6 + 2)
                pool.tensor_tensor(msq[:, :], rstd2[:, :], var[:, :], ALU.mult).then_inc(ln_pow, 1)
                pool.wait_ge(ln_pow, t * 6 + 3)
                pool.tensor_tensor(r1_sq_inv[:, :], msq[:, :], rms_eps[:, :], ALU.add).then_inc(ln_pow, 1)
                pool.wait_ge(ln_pow, t * 6 + 4)
                pool.tensor_tensor(r1[:, :], r1_sq_inv[:, :], half[:, :], ALU.pow).then_inc(ln_pow, 1)

            def keep_msq(t):
                pool.tensor_tensor(msq_eps[:, :], msq[:, :], rms_eps[:, :], ALU.add).then_inc(ln_pow, 1)

            def x_plus_b2(t):
                pool.tensor_tensor(xb[:, :, :], xin[:, :, :],
                                   b2_row[:, :].rearrange("p (a n) -> p a n", a=1).broadcast_to([P, NB, E]),
                                   ALU.add).then_inc(xb_done, 1)

            pool.wait_ge(set_mem, 6)
            inverse_root(0)
            keep_msq(0)
            pool.memset(k_stack[:, :, :, :].rearrange("p g m n -> p (g m n)").bitcast(F32), 0.0).then_inc(stack_zero, 1)
            pool.memset(q_stack[:, :, :, :, :].rearrange("p g r m n -> p (g r m n)").bitcast(F32), 0.0).then_inc(stack_zero, 1)
            def w1_lo_half(k):
                pool.wait_ge(w1_hi_done, 2 * (k + 1))
                pool.tensor_tensor(w1_lo[:, k, :], raw_w1[k], w1_hi[:, k, :].bitcast(F32),
                                   ALU.subtract).then_inc(w1_lo_done, 1)

            w1_lo_half(0)

            def body(t, more):
                def trig_q(j):
                    k = chunk_block(j)
                    later(pool, across_done, t * NB + max(j - 1, 0))
                    for r in range(2):
                        cols = r * POS + (k % 2) * P
                        row = tab[:, cols:cols + P].rearrange("p (a n) -> p a n", a=1)
                        pool.tensor_tensor(q_trig[:, j % 2, r, :, :], qT[:, :, k * P:(k + 1) * P],
                                           row.broadcast_to([P, KE, P]), ALU.mult).then_inc(q_trig_done, 1)

                pool.wait_ge(tab_in, t * 16 + 16)
                pool.wait_ge(dense_free, kq_use(t, 3) + 1)
                for i in range(2):
                    pool.wait_ge(q_stacked[i], (t + 1) * N_Q_STACK * 16)
                trig_q(0)
                pool.wait_ge(xs_done, (t + 1) * NB)
                pool.wait_ge(xn_done, (t + 1) * NB)
                pool.tensor_tensor(xn[:, :, :], xn[:, :, :],
                                   ob_row[:, :].rearrange("p (a n) -> p a n", a=1).broadcast_to([P, NB, E]),
                                   ALU.add).then_inc(xnb_done, 1)

                for j in range(NB):
                    if j + 1 < NB:
                        trig_q(j + 1)
                    if isinstance(t, int) and t == 0 and j == 0:
                        w1_lo_half(1)
                        pool.wait_ge(in_small, 16 * N_SMALL)
                        pool.wait_ge(w1_lo_done, 2)
                        x_plus_b2(0)
                    for m in range(KE):
                        n = j * KE + m
                        pool.wait_ge(upd_free, t * N_UPD + 2 + n)
                        pool.wait_ge(across_done, t * NB + j + 1)
                        later(pool, upd_used, t * NB * KE + max(n - 3, 0))
                        pool.tensor_tensor(state[:, j % B, m, :], state[:, j % B, m, :], added[:, n % 2, :],
                                           ALU.add).then_inc(upd_used, 1)
                if more:
                    inverse_root(t + 1)
                for g in range(2):
                    two = slice(2 * g, 2 * g + 2)
                    pool.wait_ge(ssq_done, t * NB + 2 * g + 2)
                    pool.tensor_tensor(ms2[:, two], mean_sq[:, two], rms_eps[:, two], ALU.add).then_inc(r2_done, 1)
                    pool.wait_ge(r2_done, t * 4 + 2 * g + 1)
                    pool.tensor_tensor(r2[:, two], ms2[:, two], half[:, two], ALU.pow).then_inc(r2_done, 1)
                pool.wait_ge(shared_free, shared_use(t, S_OUT + 1) + 1)
                later(pool, out_sent, t * 32)
                pool.tensor_tensor(res, xb[:, :, :], ctxn, ALU.add).then_inc(res_done, 1)
                pool.wait_ge(ffn_done, (t + 1) * NB)
                pool.wait_ge(res_done, t * 2 + 1)
                pool.tensor_tensor(res, res, ctxn, ALU.add).then_inc(res_done, 1)
                if more:
                    keep_msq(t + 1)
                    pool.wait_ge(x_in, t * 32 + 64)
                    x_plus_b2(t + 1)

            body(0, True)
            with pool.Fori(1, NT - 1) as t:
                body(t, True)
            body(NT - 1, False)

        @block.scalar
        def _(act):
            smalls = [
                (v_raw, v, in_fb),
                (fbT, fast_b.rearrange("r k -> k r"), in_fb),
                (qkb[:, :], qkv_b[0:2 * E].rearrange("(k p) -> p k", p=P), in_small),
                (n2w[:, :], norm2_w.rearrange("(k p) -> p k", p=P), in_small),
                (u_raw, u.rearrange("(m p) r -> p m r", p=P), in_small),
                (gate_col[:, :], gate.broadcast_to([P, 1]), in_small),
                (vb_row[:, :], qkv_b[2 * E:3 * E].rearrange("(a n) -> a n", a=1).broadcast_to([P, E]), in_small),
                (b2_row[:, :], mlp_b2.rearrange("(a n) -> a n", a=1).broadcast_to([P, E]), in_small),
                (ob_row[:, :], out_b.rearrange("(a n) -> a n", a=1).broadcast_to([P, E]), in_small),
                (b1[:, :], mlp_b1.rearrange("(k p) -> p k", p=P), in_small),
            ]
            assert len(smalls) == N_SMALL + 2
            for dst, src, landed in smalls:
                act.dma_start(dst, src, allow_slow_non_contiguous=True).then_inc(landed, 16)

            def z_hi(t):
                act.wait_ge(upd_full, t * N_UPD + 1)
                act.activation(z_st[:, :], upd_ps[:, :], ACT.Copy).then_inc(z_hi_done, 1)

            def w1_hi_half(k):
                act.wait_ge(in_w1[k], 16)
                act.activation(raw_w1[k], raw_w1[k], ACT.Copy, scale=n2w[:, k:k + 1]).then_inc(w1_hi_done, 1)
                act.wait_ge(w1_hi_done, 2 * k + 1)
                act.activation(w1_hi[:, k, :], raw_w1[k], ACT.Copy).then_inc(w1_hi_done, 1)

            def sum_abs(raw, load, base, count, width):
                act.wait_ge(load, 16)
                for m in range(count):
                    if base + m >= 2:
                        act.wait_ge(sums_done, base + m - (0 if width > E else 1))
                    act.activation(junk[:, (m % 2) * E:(m % 2) * E + width] if width == E else junk, raw[:, m, :],
                                   ACT.Abs, accum_out=sums[:, base + m:base + m + 1]).then_inc(sums_done, 1)

            def scale_x(t):
                act.wait_ge(ln_pow, t * 6 + 5)
                for k in range(NB):
                    act.wait_ge(xn_done, t * NB + k + 1)
                    act.activation(xs[:, k, :], xn[:, k, :], ACT.Copy, scale=r1[:, k:k + 1]).then_inc(xs_done, 1)

            def x_hi(t):
                for m in range(KE):
                    act.wait_ge(shared_full, shared_use(t, m - KE) + 1)
                    act.activation(xT_hi[:, m, :], shared[m][:, :], ACT.Copy).then_inc(xT_hi_done, 1)

            def relu_kq(t):
                if not isinstance(t, int) or t:
                    act.wait_ge(q_trig_done, t * 2 * NB)
                for i, (dst, base) in enumerate(((kT, KE), (qT, 0))):
                    for m in range(KE):
                        act.wait_ge(dense_full, kq_use(t, i * KE + m) + 1)
                        act.activation(dst[:, m, :], dense[m][:, :], ACT.Relu,
                                       bias=qkb[:, base + m:base + m + 1]).then_inc(dense_free, 1)

            scale_x(0)
            x_hi(0)
            act.wait_ge(zw_full, 1)
            act.activation(zw[:, :, :].rearrange("p k n -> p (k n)"), upd_ps[:, 0:KE * P], ACT.Copy).then_inc(zw_done, 1)
            sum_abs(raw_fc, in_fc, 0, HB, E)
            act.wait_ge(in_small, 16 * N_SMALL)
            relu_kq(0)
            act.wait_ge(fc_tern, HB)
            sum_abs(raw_pr, in_pr, HB, KE, HID)

            def read(n, dst, bank):
                act.wait_ge(set_pe, n + 1)
                act.activation(dst, bank, ACT.Copy).then_inc(read_out, 1)

            for m in range(KE):
                for g in range(2):
                    read(SET_FC + m * 2 + g, fcT[:, m, g * TOK:(g + 1) * TOK], (dense + accum)[m * 2 + g][:, :])
            w1_hi_half(0)
            for g in range(2):
                read(SET_G + g, gT[:, g * TOK:(g + 1) * TOK], dense[g][:, :])
            act.dma_start(raw_w1[1], mlp_w1[P:2 * P, :]).then_inc(in_w1[1], 16)
            read(SET_SC, pr_scale_row[:, :], ctx_ps[:, 0:E])
            for g in range(4):
                read(SET_PR + g, prT[:, 2 * g:2 * g + 2, :].rearrange("p h n -> p (h n)"), (dense + accum)[g][:, :])
            z_hi(0)
            act.wait_ge(set_pe, SET_ALL)
            act.dma_start(raw_w2, mlp_w2.rearrange("(k p) n -> p k n", p=P)).then_inc(in_w2, 16)

            def body(t, more):
                def ffn_block(m):
                    act.wait_ge(dense_full, dense_use(t, m) + 1)
                    later(act, wide_used, t * 2 * HB + max(m - 1, 0))
                    act.activation(wide[:, m % 2, :], dense[m % 2][:, :], ACT.Relu,
                                   scale=scales[:, m:m + 1]).then_inc(dense_free, 1)
                    act.wait_ge(dense_free, dense_use(t, m) + 1)
                    act.activation(wide[:, m % 2, :], wide[:, m % 2, :], ACT.Square).then_inc(wide_done, 1)

                def mlp_block(m):
                    act.wait_ge(dense_full, mlp_use(t, m, more) + 1)
                    act.wait_ge(wide_used, t * 2 * HB + HB + m - 1)
                    act.activation(wide[:, m % 2, :], dense[m % 2][:, :], ACT.Gelu_apprx_tanh,
                                   bias=b1[:, m:m + 1]).then_inc(dense_free, 1)

                def trig_v(j):
                    k = chunk_block(j)
                    act.wait_ge(shared_free, shared_use(t, S_V + k // 2) + 1)
                    later(act, upd_full, t * N_UPD + max(2 * j - 1, 0))
                    for r in range(2):
                        c = 2 * POS + 2 * r + k % 2
                        act.activation(v_trig[:, j % 2, :, r, :],
                                       v_tok[:, k, :, :].rearrange("p (m h) e -> p m (h e)", m=KE),
                                       ACT.Copy, scale=tab[:, c:c + 1]).then_inc(v_trig_done, 1)

                ffn_block(0)
                for g in range(2):
                    act.wait_ge(k_turned, t * 2 + g + 1)
                    act.activation(k_tok[:, 2 * g:2 * g + 2, :].rearrange("p b n -> p (b n)"), accum[g][:, :],
                                   ACT.Copy).then_inc(k_tok_done, 1)
                ffn_block(1)
                act.wait_ge(tab_in, t * 16 + 16)
                for i in range(2):
                    act.wait_ge(q_stacked[i], (t + 1) * N_Q_STACK * 16)
                trig_v(0)
                if isinstance(t, int) and t == 0:
                    w1_hi_half(1)
                for j in range(NB):
                    if j + 1 < NB:
                        trig_v(j + 1)
                    ffn_block(j + 2)
                for m in range(KE):
                    act.wait_ge(shared_full, shared_use(t, S_CT + m) + 1)
                    act.activation(cT_hi[:, m, :], shared[m][:, :], ACT.Copy).then_inc(cT_hi_done, 1)
                ffn_block(6)
                for k in range(NB):
                    act.wait_ge(shared_free, shared_use(t, S_OUT + k // 2) + 1)
                    act.activation(xs[:, k, :], ctxn[:, k, :], ACT.Square, scale=float(E) ** -0.5,
                                   accum_out=mean_sq[:, k:k + 1]).then_inc(ssq_done, 1)
                ffn_block(7)
                for m in range(KE):
                    act.wait_ge(shared_full, shared_use(t, S_HT + m) + 1)
                    act.activation(cT_hi[:, m, :], shared[m][:, :], ACT.Copy).then_inc(cT_hi_done, 1)
                if more:
                    scale_x(t + 1)
                for m in range(HB):
                    mlp_block(m)
                    if m == 0 and more:
                        x_hi(t + 1)
                    if m == MLP_BEFORE_KQ - 1 and more:
                        relu_kq(t + 1)
                if more:
                    z_hi(t + 1)

            body(0, True)
            with act.Fori(1, NT - 1) as t:
                body(t, True)
            body(NT - 1, False)

        @block.vector
        def _(dve):
            def ln_statistics(t):
                dve.wait_ge(x_in, t * 32 + 32)
                later(dve, ln_pow, t * 6)
                for k in range(NB):
                    dve.bn_stats(stats[:, k, :], xin[:, k, :]).then_inc(ln_stats, 1)

            def moments(t):
                base = t * N_STATS
                dve.wait_ge(ln_stats, base + NB)
                for dst, col, op in ((mean_sum, 1, ALU.add), (mean_dif, 1, ALU.subtract), (var_sum, 2, ALU.add)):
                    dve.tensor_tensor(dst[:, :], stats[:, :, col], stats[:, :, 3 + col], op).then_inc(ln_stats, 1)
                dve.wait_ge(ln_stats, base + NB + 3)
                dve.scalar_tensor_tensor(dif_sq[:, :], mean_dif[:, :], 0.25, mean_dif[:, :],
                                         ALU.mult, ALU.mult).then_inc(ln_stats, 1)
                dve.tensor_scalar(mean[:, :], mean_sum[:, :], 0.5, None, ALU.mult).then_inc(ln_stats, 1)
                dve.wait_ge(ln_stats, base + NB + 5)
                dve.scalar_tensor_tensor(var[:, :], var_sum[:, :], 1.0 / E, dif_sq[:, :],
                                         ALU.mult, ALU.add).then_inc(ln_stats, 1)
                dve.wait_ge(ln_stats, base + NB + 6)
                dve.tensor_scalar(var_eps[:, :], var[:, :], LN_EPS, None, ALU.add).then_inc(ln_stats, 1)

            def layernorm(t):
                dve.wait_ge(ln_pow, t * 6 + 1)
                for k in range(NB):
                    dve.tensor_scalar(xn[:, k, :], xin[:, k, :], mean[:, k:k + 1], rstd[:, k:k + 1],
                                      ALU.subtract, ALU.mult).then_inc(xn_done, 1)

            def x_lo(t):
                for m in range(KE):
                    dve.wait_ge(xT_hi_done, t * KE + m + 1)
                    dve.tensor_tensor(xT_lo[:, m, :], shared[m][:, :], xT_hi[:, m, :].bitcast(F32),
                                      ALU.subtract).then_inc(shared_free, 1)

            def split_weight(src, load, hi, lo, done, scale=None):
                steps = 0
                dve.wait_ge(load, 16)
                if scale is not None:
                    for k in range(KE):
                        dve.tensor_scalar(src[:, k, :], src[:, k, :], scale[:, k:k + 1], None, ALU.mult).then_inc(done, 1)
                        steps += 1
                    dve.wait_ge(done, steps)
                dve.tensor_copy(hi[:, :, :], src).then_inc(done, 1)
                dve.wait_ge(done, steps + 1)
                dve.tensor_tensor(lo[:, :, :], src, hi[:, :, :].bitcast(F32), ALU.subtract).then_inc(done, 1)

            def split_parts(t, src, parts, use, done):
                for m in range(KE):
                    dve.wait_ge(dense_free, kq_use(t, use + m) + 1)
                    dve.tensor_copy(parts[:, 0, m, :].bitcast(F32R), src[:, m, :]).then_inc(done, 1)
                    dve.wait_ge(done, t * 2 * KE + 2 * m + 1)
                    dve.tensor_tensor(parts[:, 1, m, :].bitcast(F32R), src[:, m, :], parts[:, 0, m, :],
                                      ALU.subtract).then_inc(done, 1)

            def k_parts_split(t):
                if not isinstance(t, int) or t:
                    dve.wait_ge(av_done, t * 4 * NB)
                split_parts(t, kT, k_parts, 0, k_parts_done)

            def q_parts_split(t):
                split_parts(t, qT, q_parts, KE, q_parts_done)

            def v_rows(t, g):
                later(dve, v_trig_done, t * 2 * NB)
                dve.wait_ge(shared_full, shared_use(t, S_V + g) + 1)
                made = shared[g][:, :].rearrange("p (b h e) -> p b h e", b=2, h=H)
                bias = vb_row[:, :].rearrange("p (a h e) -> p a h e", a=1, h=H).broadcast_to([P, 2, H, D])
                dve.tensor_tensor(v_tok[:, 2 * g:2 * g + 2, :, 0:D], made, bias, ALU.add).then_inc(shared_free, 1)

            def w2_quarter(i):
                two = slice(2 * i, 2 * i + 2)
                dve.wait_ge(in_w2, 16)
                dve.tensor_copy(w2_hi[:, two, :], raw_w2[:, two, :]).then_inc(w2_split, 1)
                dve.wait_ge(w2_split, 2 * i + 1)
                dve.tensor_tensor(w2_lo[:, two, :], raw_w2[:, two, :], w2_hi[:, two, :].bitcast(F32),
                                  ALU.subtract).then_inc(w2_split, 1)

            def z_lo(t):
                dve.wait_ge(z_hi_done, t + 1)
                dve.tensor_tensor(z_st[64:96, :], upd_ps[64:96, :], z_st[64:96, :].bitcast(F32),
                                  ALU.subtract).then_inc(upd_free, 1)

            ln_statistics(0)
            moments(0)
            layernorm(0)
            dve.wait_ge(in_n1, 16)
            split_weight(raw_qkv, in_qkv, wqkv_hi, wqkv_lo, qkv_split, n1w)
            dve.wait_ge(in_fb, 32)
            dve.wait_ge(set_mem, 6)
            dve.tensor_copy(fb4[:, :, 0:RANK], fbT.rearrange("p (a r) -> p a r", a=1).broadcast_to([RANK, 4, RANK])
                            ).then_inc(fb_done, 1)
            x_lo(0)
            dve.wait_ge(zw_done, 1)
            lo_part = zw[:, :, 96:128]
            dve.tensor_tensor(lo_part, upd_ps[:, 0:KE * P].rearrange("p (k n) -> p k n", k=KE)[:, :, 96:128],
                              lo_part.bitcast(F32), ALU.subtract).then_inc(zw_done, 1)
            split_weight(raw_wo, in_wo, wo_hi, wo_lo, wo_split)
            n = 0
            def scale_columns(n, lo_c, hi_c, count):
                dve.wait_ge(sums_done, hi_c)
                dve.tensor_scalar(scales[:, lo_c:hi_c], sums[:, lo_c:hi_c], 1.0 / count, 1e-5,
                                  ALU.mult, ALU.max).then_inc(set_dve, 1)
                dve.wait_ge(set_dve, n + 1)
                dve.tensor_scalar(half_pos[:, lo_c:hi_c], scales[:, lo_c:hi_c], 0.5, None, ALU.mult).then_inc(set_dve, 1)
                dve.tensor_scalar(half_neg[:, lo_c:hi_c], scales[:, lo_c:hi_c], -0.5, None, ALU.mult).then_inc(set_dve, 1)
                return n + 3

            n = scale_columns(n, 0, HB, E)
            dve.reciprocal(g_by_s[:, :], scales[:, 0:HB]).then_inc(set_dve, 1)
            n += 1
            for m in range(HB):
                if m == 2:
                    k_parts_split(0)
                dve.wait_ge(set_dve, n)
                dve.tensor_scalar(less[:, m % 2, 0:E], raw_fc[:, m, :], half_neg[:, m:m + 1], None,
                                  ALU.is_lt).then_inc(set_dve, 1)
                n += 1
                dve.wait_ge(set_dve, n)
                dve.scalar_tensor_tensor(raw_fc[:, m, :], raw_fc[:, m, :], half_pos[:, m:m + 1], less[:, m % 2, 0:E],
                                         ALU.is_gt, ALU.subtract).then_inc(fc_tern, 1)
            q_parts_split(0)
            dve.wait_ge(in_small, 16 * N_SMALL)
            dve.tensor_scalar(g_by_s[:, :], g_by_s[:, :], gate_col[:, 0:1], None, ALU.mult).then_inc(set_dve, 1)
            n += 1
            dve.wait_ge(set_dve, n)
            for q in range(4):
                dve.tensor_tensor(u4[:, :, q, 0:RANK], u_raw,
                                  g_by_s[:, :].rearrange("p (m a) -> p m a", a=1).broadcast_to([P, HB, RANK]),
                                  ALU.mult).then_inc(u4_done, 1)
            n = scale_columns(n, HB, HB + KE, HID)
            dve.wait_ge(set_dve, n)
            dve.wait_ge(fc_tern, HB)
            dve.wait_ge(zw_full, 1)
            dve.wait_ge(in_const, 16)
            for m in range(KE):
                both = less[:, :, :].rearrange("p a n -> p (a n)")
                c = HB + m
                dve.wait_ge(pr_tern, m)
                dve.tensor_scalar(both, raw_pr[:, m, :], half_neg[:, c:c + 1], None, ALU.is_lt).then_inc(set_dve, 1)
                n += 1
                dve.wait_ge(set_dve, n)
                dve.scalar_tensor_tensor(raw_pr[:, m, :], raw_pr[:, m, :], half_pos[:, c:c + 1], both,
                                         ALU.is_gt, ALU.subtract).then_inc(pr_tern, 1)
                dve.tensor_scalar(diag_scale[:, m, :], ident, scales[:, c:c + 1], None, ALU.mult).then_inc(diag_done, 1)
            for g in range(2):
                dve.wait_ge(read_out, SET_G + g + 1)
                part = gT[32:64, g * TOK:(g + 1) * TOK]
                dve.tensor_tensor(part, dense[g][32:64, :], part.bitcast(F32), ALU.subtract).then_inc(g_lo_done, 1)
            dve.wait_ge(set_pe, SET_FC + 4)
            dve.memset(v_tok[:, :, :, D:VW].rearrange("p b h e -> p (b h) e"), 1.0).then_inc(ones_done, 1)
            dve.wait_ge(ones_done, 1)
            v_rows(0, 0)
            z_lo(0)
            dve.wait_ge(read_out, SET_SC + 1)

            def body(t, more):
                def split(n):
                    if n < HB:
                        dve.wait_ge(wide_done, t * HB + n + 1)
                    else:
                        dve.wait_ge(dense_free, mlp_use(t, n - HB, more) + 1)
                    dve.tensor_copy(wide_hi[:, n % 2, :], wide[:, n % 2, :]).then_inc(hi_done, 1)
                    dve.wait_ge(hi_done, t * 2 * HB + n + 1)
                    dve.tensor_tensor(wide_lo[:, n % 2, :], wide[:, n % 2, :], wide_hi[:, n % 2, :].bitcast(F32),
                                      ALU.subtract).then_inc(lo_done, 1)

                def weigh(j, g):
                    i = 4 * j + g
                    dve.wait_ge(shared_full, shared_use(t, S_SCORE + i) + 1)
                    later(dve, av_done, t * 4 * NB + max(i - 3, 0))
                    dve.tensor_tensor(weighted[:, g, :].rearrange("p (a n) -> p a n", a=4),
                                      shared[g % 2][:, :].rearrange("p (a n) -> p a n", a=4),
                                      mask.rearrange("p (a n) -> p a n", a=1).broadcast_to([P, 4, P]),
                                      ALU.mult).then_inc(shared_free, 1)

                def context(j):
                    heads = ctx_ps[:, 0:H * VW].rearrange("p (h e) -> p h e", e=VW)
                    c = t * 2 * NB + 2 * j
                    dve.wait_ge(av_done, (t * NB + j + 1) * 4)
                    dve.tensor_scalar(norm[:, :], heads[:, :, D], NORM_EPS, None, ALU.add).then_inc(norm_done, 1)
                    dve.wait_ge(norm_done, c + 1)
                    dve.reciprocal(recip[:, :], norm[:, :]).then_inc(norm_done, 1)
                    dve.wait_ge(norm_done, c + 2)
                    if j == 0:
                        later(dve, res_done, t * 2)
                    dve.tensor_tensor(ctxn[:, chunk_block(j), :].rearrange("p (h e) -> p h e", e=D), heads[:, :, 0:D],
                                      recip[:, :].rearrange("p (h a) -> p h a", a=1).broadcast_to([P, H, D]),
                                      ALU.mult).then_inc(ctx_free, 1)

                def mask_update(j, m):
                    n = j * KE + m
                    dve.wait_ge(upd_full, t * N_UPD + 2 + n)
                    later(dve, upd_used, t * NB * KE + max(n - 1, 0))
                    dve.tensor_tensor(added[:, n % 2, :], upd_ps[:, 0:2 * HW], diag, ALU.mult).then_inc(upd_free, 1)

                v_rows(t, 1)
                split(0)
                dve.wait_ge(k_stacked, (t + 1) * N_K_STACK * 16)
                weigh(0, 0)
                weigh(0, 1)
                for j in range(NB):
                    setting_up = isinstance(t, int) and t == 0 and j == 0
                    weigh(j, 2)
                    if setting_up:
                        w2_quarter(0)
                    split(j + 1)
                    if setting_up:
                        w2_quarter(1)
                    weigh(j, 3)
                    if setting_up:
                        w2_quarter(2)
                    mask_update(j, 0)
                    if setting_up:
                        w2_quarter(3)
                    if j + 1 < NB:
                        weigh(j + 1, 0)
                    context(j)
                    if j + 1 < NB:
                        weigh(j + 1, 1)
                    mask_update(j, 1)
                    if j == 1 and more:
                        ln_statistics(t + 1)
                    if j == 2 and more:
                        moments(t + 1)
                for m in range(KE):
                    dve.wait_ge(cT_hi_done, t * 2 * KE + m + 1)
                    dve.tensor_tensor(cT_lo[:, m, :], shared[m][:, :], cT_hi[:, m, :].bitcast(F32),
                                      ALU.subtract).then_inc(shared_free, 1)
                split(5)
                split(6)
                dve.wait_ge(xnb_done, t + 1)
                for g in range(2):
                    dve.wait_ge(shared_full, shared_use(t, S_OUT + g) + 1)
                    dve.tensor_tensor(ctxn[:, 2 * g:2 * g + 2, :].rearrange("p b n -> p (b n)"), shared[g][:, :],
                                      xn[:, 2 * g:2 * g + 2, :].rearrange("p b n -> p (b n)"), ALU.add).then_inc(shared_free, 1)
                if more:
                    dve.wait_ge(shared_free, shared_use(t, S_OUT + 1) + 1)
                    layernorm(t + 1)
                for k in range(NB):
                    dve.wait_ge(r2_done, t * 4 + k // 2 * 2 + 2)
                    dve.tensor_scalar(xs[:, k, :], ctxn[:, k, :], r2[:, k:k + 1], None, ALU.mult).then_inc(hs_done, 1)
                split(7)
                for m in range(KE):
                    dve.wait_ge(cT_hi_done, t * 2 * KE + KE + m + 1)
                    dve.tensor_tensor(cT_lo[:, m, :], shared[m][:, :], cT_hi[:, m, :].bitcast(F32),
                                      ALU.subtract).then_inc(shared_free, 1)
                dve.wait_ge(wide_used, t * 2 * HB + HB)
                dve.wait_ge(res_done, t * 2 + 1)
                for k in range(NB):
                    dve.scalar_tensor_tensor(ctxn[:, k, :], accum[k // 2][:, (k % 2) * E:(k % 2 + 1) * E],
                                             msq_eps[:, k:k + 1], pr_scale_row[:, :],
                                             ALU.mult, ALU.mult).then_inc(ffn_done, 1)
                for m in range(HB):
                    split(HB + m)
                    if m == 0 and more:
                        x_lo(t + 1)
                    if m == MLP_BEFORE_KQ - 1 and more:
                        k_parts_split(t + 1)
                        q_parts_split(t + 1)
                if more:
                    z_lo(t + 1)
                    v_rows(t + 1, 0)
                dve.wait_ge(res_done, t * 2 + 2)
                dve.wait_ge(wide_used, (t + 1) * 2 * HB)
                for g in range(2):
                    dve.tensor_tensor(res[:, 2 * g:2 * g + 2, :].rearrange("p b n -> p (b n)"), accum[g][:, :],
                                      res[:, 2 * g:2 * g + 2, :].rearrange("p b n -> p (b n)"), ALU.add).then_inc(out_done, 1)

            body(0, True)
            with dve.Fori(1, NT - 1) as t:
                body(t, True)
            body(NT - 1, False)

        @block.tensor
        def _(pe):
            def turn_x(t):
                pe.wait_ge(xs_done, (t + 1) * NB)
                for m in range(KE):
                    use = shared_use(t, m - KE)
                    if not isinstance(t, int) or t:
                        pe.wait_ge(shared_free, use - 1)
                    for k in range(NB):
                        mm = pe.transpose(shared[m][:, k * P:(k + 1) * P], xs[:, k, m * P:(m + 1) * P], ident)
                    mm.then_inc(shared_full, 1)

            def dense_bank(use, n):
                later(pe, dense_free, use - 1)
                return dense[n % 2]

            def product3(dst, w_hi, w_lo, a_hi, a_lo, cols):
                for k in range(KE):
                    for i, (w, a) in enumerate(((w_hi, a_hi), (w_hi, a_lo), (w_lo, a_hi))):
                        mm = pe.matmul(dst, w[:, k, cols], a[:, k, :], start=(k == 0 and i == 0),
                                       stop=(k == KE - 1 and i == 2))
                return mm

            def make_kq(t):
                pe.wait_ge(shared_free, shared_use(t, -1) + 1)
                for i, base in enumerate((E, E + P, 0, P)):
                    bank = dense_bank(kq_use(t, i), i)
                    product3(bank[:, :], wqkv_hi, wqkv_lo, xT_hi, xT_lo,
                             slice(base, base + P)).then_inc(dense_full, 1)

            def make_v(t, g):
                pe.wait_ge(shared_free, shared_use(t, S_V + g) - 1)
                for i in range(2):
                    tok = slice((2 * g + i) * P, (2 * g + i + 1) * P)
                    for k in range(KE):
                        for c, (a, w) in enumerate(((xT_hi, wqkv_hi), (xT_hi, wqkv_lo), (xT_lo, wqkv_hi))):
                            mm = pe.matmul(shared[g][:, i * E:(i + 1) * E], a[:, k, tok], w[:, k, 2 * E:3 * E],
                                           start=(k == 0 and c == 0), stop=(k == KE - 1 and c == 2))
                mm.then_inc(shared_full, 1)

            def make_z(t):
                later(pe, upd_free, t * N_UPD)
                for k in range(KE):
                    for a in (xT_hi, xT_lo):
                        mm = pe.matmul(upd_ps[:, :], zw[:, k, :], a[:, k, :], start=(k == 0 and a is xT_hi),
                                       stop=(k == KE - 1 and a is xT_lo))
                mm.then_inc(upd_full, 1)

            pe.wait_ge(in_const, 16)
            turn_x(0)
            pe.wait_ge(fb_done, 1)
            for m in range(KE):
                mm = pe.matmul(upd_ps[:, m * P:(m + 1) * P], v_raw[:, m * P:(m + 1) * P],
                               fb4.rearrange("p q r -> p (q r)"), start=True, stop=True)
            mm.then_inc(zw_full, 1)
            pe.wait_ge(qkv_split, KE + 2)
            make_kq(0)
            pe.wait_ge(dense_free, 2 * KE)
            pe.wait_ge(fc_tern, HB)
            for m in range(KE):
                for g in range(2):
                    for i in range(4):
                        mm = pe.transpose((dense + accum)[m * 2 + g][:, i * P:(i + 1) * P],
                                          raw_fc[:, 4 * g + i, m * P:(m + 1) * P], ident)
                    mm.then_inc(set_pe, 1)
            pe.wait_ge(u4_done, 4)
            pe.wait_ge(read_out, SET_FC + 2)
            for g in range(2):
                for i in range(4):
                    mm = pe.transpose(dense[g][:, i * P:(i + 1) * P],
                                      u4[:, 4 * g + i, :, :].rearrange("p q r -> p (q r)"), ident)
                mm.then_inc(set_pe, 1)
            pe.wait_ge(set_mem, 6)
            pe.wait_ge(diag_done, KE)
            pe.matmul(ctx_ps[:, 0:E], ones[:, :], diag_scale.rearrange("p k n -> p (k n)"),
                      start=True, stop=True).then_inc(set_pe, 1)
            pe.wait_ge(pr_tern, KE)
            pe.wait_ge(g_lo_done, 2)
            pe.wait_ge(read_out, SET_G + 2)
            for g in range(4):
                for hb in range(2):
                    for m in range(KE):
                        mm = pe.transpose((dense + accum)[g][:, hb * E + m * P:hb * E + (m + 1) * P],
                                          raw_pr[:, m, (2 * g + hb) * P:(2 * g + hb + 1) * P], ident)
                mm.then_inc(set_pe, 1)
            pe.wait_ge(read_out, SET_ALL)
            pe.wait_ge(ones_done, 1)
            pe.wait_ge(zw_done, 2)
            pe.wait_ge(q_stacked[0], N_Q_STACK * 16)
            make_v(0, 0)
            make_z(0)

            def body(t, more):
                def shared_bank(n):
                    pe.wait_ge(shared_free, shared_use(t, n) - 1)
                    return shared[n % 2]

                def ffn_up(m, steps=range(5)):
                    bank = dense[m % 2]
                    cols = slice(m * P, (m + 1) * P)
                    for i in steps:
                        if i == 0:
                            dense_bank(dense_use(t, m), m)
                        if i < 4:
                            pe.matmul(bank[:, :], fcT[:, i // 2, cols], (xT_hi, xT_lo)[i % 2][:, i // 2, :],
                                      start=(i == 0), stop=False)
                        else:
                            if m == 0:
                                pe.wait_ge(upd_free, t * N_UPD + 1)
                            pe.matmul(bank[:, :], gT[:, cols], z_st[:, :], start=False, stop=True).then_inc(dense_full, 1)

                def down(n, pairs, blocks):
                    first, last = n % HB == 0, n % HB == HB - 1
                    pe.wait_ge(lo_done, t * 2 * HB + n + 1)
                    for k in blocks:
                        tok = slice(k * P, (k + 1) * P)
                        for i, (a, w) in enumerate(pairs):
                            mm = pe.matmul(accum[k // 2][:, (k % 2) * E:(k % 2 + 1) * E], a[:, n % 2, tok],
                                           w[:, n % HB, :], start=(first and i == 0 and k % 2 == 0),
                                           stop=(last and i == len(pairs) - 1), skip_group_check=True)
                    if blocks[-1] == NB - 1:
                        mm.then_inc(wide_used, 1)

                def ffn_down(m, blocks=range(NB)):
                    if m == 0 and blocks[0] == 0:
                        pe.wait_ge(k_tok_done, t * 2 + 2)
                    down(m, ((wide_hi, prT), (wide_lo, prT)), blocks)

                def scores(j, g):
                    bank = shared_bank(S_SCORE + 4 * j + g)
                    tok = slice(chunk_block(j) * P, (chunk_block(j) + 1) * P)
                    if j == 0 and g == 0:
                        pe.wait_ge(k_stacked, (t + 1) * N_K_STACK * 16)
                    if j == 0 and g % 2 == 0:
                        pe.wait_ge(q_stacked[g // 2], (t + 1) * N_Q_STACK * 16)
                    for i in range(2):
                        row, m = g // 2 * 2 + i, g % 2
                        mm = pe.matmul(bank[:, i * 2 * P:(i + 1) * 2 * P].rearrange("p (r n) -> p r n", r=2),
                                       k_stack[:, row, m, tok], q_stack[:, row, :, m, tok], start=True, stop=True)
                    mm.then_inc(shared_full, 1)

                def within(j, g, half):
                    k = chunk_block(j)
                    if g == 0 and half == 0:
                        later(pe, ctx_free, t * NB + j)
                    pe.wait_ge(shared_free, shared_use(t, S_SCORE + 4 * j + g) + 1)
                    for i in (2 * half, 2 * half + 1):
                        h = g % 2 * (H // KE) + g // 2 * 4 + i
                        mm = pe.matmul(ctx_ps[:, h * VW:(h + 1) * VW], weighted[:, g, i * P:(i + 1) * P],
                                       v_tok[:, k, h, :], start=(g == 0 and i == 0), stop=(g == 3 and i == 3),
                                       skip_group_check=True)
                    if half:
                        mm.then_inc(av_done, 1)

                def across(j, m):
                    pe.wait_ge(q_trig_done, t * 2 * NB + 2 * (j + 1))
                    later(pe, upd_used, t * NB * KE + max(j - 1, 0) * KE)
                    for r in range(2):
                        mm = pe.matmul(ctx_ps[:, m * HW:(m + 1) * HW], q_trig[:, j % 2, r, m, :],
                                       state[:, j % B, m, r * HW:(r + 1) * HW], start=False, stop=False,
                                       skip_group_check=True)
                    if m == KE - 1:
                        mm.then_inc(across_done, 1)

                def update(j, m):
                    k = chunk_block(j)
                    pe.wait_ge(upd_free, t * N_UPD + 1 + j * KE + m)
                    if j == 0:
                        pe.wait_ge(k_tok_done, t * 2 + 2)
                    pe.wait_ge(v_trig_done, t * 2 * NB + 2 * (j + 1))
                    pe.matmul(upd_ps[:, 0:2 * HW], k_tok[:, k, m * P:(m + 1) * P],
                              v_trig[:, j % 2, m, :, :].rearrange("p r n -> p (r n)"),
                              start=True, stop=True).then_inc(upd_full, 1)

                ffn_up(0)
                make_v(t, 1)
                later(pe, out_done, t * 2)
                pe.wait_ge(dense_free, kq_use(t, KE - 1) + 1)
                for g in range(2):
                    for i in range(2):
                        for m in range(KE):
                            mm = pe.transpose(accum[g][:, i * E + m * P:i * E + (m + 1) * P],
                                              kT[:, m, (2 * g + i) * P:(2 * g + i + 1) * P], ident)
                    mm.then_inc(k_turned, 1)
                scores(0, 0)
                scores(0, 1)
                ffn_up(1)
                for j in range(NB):
                    scores(j, 2)
                    within(j, 0, 0)
                    ffn_down(j, (0,))
                    within(j, 0, 1)
                    ffn_down(j, (1,))
                    across(j, 0)
                    scores(j, 3)
                    within(j, 1, 0)
                    ffn_down(j, (2,))
                    within(j, 1, 1)
                    ffn_down(j, (3,))
                    update(j, 0)
                    if j + 1 < NB:
                        scores(j + 1, 0)
                    within(j, 2, 0)
                    ffn_up(j + 2, (0,))
                    within(j, 2, 1)
                    ffn_up(j + 2, (1,))
                    across(j, 1)
                    ffn_up(j + 2, (2,))
                    within(j, 3, 0)
                    ffn_up(j + 2, (3,))
                    within(j, 3, 1)
                    if j + 1 < NB:
                        scores(j + 1, 1)
                    update(j, 1)
                    ffn_up(j + 2, (4,))
                ffn_down(4, (0, 1))
                pe.wait_ge(ctx_free, t * NB + NB)
                for m in range(KE):
                    bank = shared_bank(S_CT + m)
                    for k in range(NB):
                        mm = pe.transpose(bank[:, k * P:(k + 1) * P], ctxn[:, k, m * P:(m + 1) * P], ident)
                    mm.then_inc(shared_full, 1)
                ffn_up(6)
                ffn_down(4, (2, 3))
                if isinstance(t, int) and t == 0:
                    pe.wait_ge(wo_split, 2)
                for g in range(2):
                    bank = shared_bank(S_OUT + g)
                    for part, a, ws in ((0, cT_hi, (wo_hi, wo_lo)), (1, cT_lo, (wo_hi,))):
                        if g == 0:
                            if part == 0:
                                pe.wait_ge(cT_hi_done, t * 2 * KE + KE)
                            else:
                                pe.wait_ge(shared_free, shared_use(t, S_CT + 1) + 1)
                        for i in range(2):
                            tok = slice((2 * g + i) * P, (2 * g + i + 1) * P)
                            for k in range(KE):
                                for c, w in enumerate(ws):
                                    mm = pe.matmul(bank[:, i * E:(i + 1) * E], a[:, k, tok], w[:, k, :],
                                                   start=(part == 0 and i == 0 and k == 0 and c == 0),
                                                   stop=(part == 1 and k == KE - 1), skip_group_check=True)
                    mm.then_inc(shared_full, 1)
                ffn_down(5)
                ffn_up(7)
                ffn_down(6)
                banks = [shared_bank(S_HT + m) for m in range(KE)]
                for k in range(NB):
                    pe.wait_ge(hs_done, t * NB + k + 1)
                    for m in range(KE):
                        mm = pe.transpose(banks[m][:, k * P:(k + 1) * P], xs[:, k, m * P:(m + 1) * P], ident)
                        if k == NB - 1:
                            mm.then_inc(shared_full, 1)
                ffn_down(7)

                def mlp_up(m):
                    bank = dense_bank(mlp_use(t, m, more), m)
                    cols = slice(m * P, (m + 1) * P)
                    for k in range(KE):
                        if m == 0:
                            pe.wait_ge(cT_hi_done, t * 2 * KE + KE + k + 1)
                        for i, w in enumerate((w1_hi, w1_lo)):
                            pe.matmul(bank[:, :], w[:, k, cols], cT_hi[:, k, :], start=(k == 0 and i == 0), stop=False)
                    for k in range(KE):
                        if m == 0:
                            pe.wait_ge(shared_free, shared_use(t, S_HT + k) + 1)
                        mm = pe.matmul(bank[:, :], w1_hi[:, k, cols], cT_lo[:, k, :], start=False, stop=(k == KE - 1))
                    mm.then_inc(dense_full, 1)

                def mlp_down(m):
                    if m == 0:
                        pe.wait_ge(ffn_done, (t + 1) * NB)
                    down(HB + m, ((wide_hi, w2_hi), (wide_hi, w2_lo), (wide_lo, w2_hi)), range(NB))

                if isinstance(t, int) and t == 0:
                    pe.wait_ge(w1_lo_done, KE)
                    pe.wait_ge(w2_split, 8)
                mlp_up(0)
                if more:
                    turn_x(t + 1)
                for m in range(1, HB):
                    mlp_up(m)
                    mlp_down(m - 1)
                    if m == MLP_BEFORE_KQ - 1 and more:
                        make_kq(t + 1)
                if more:
                    make_z(t + 1)
                    make_v(t + 1, 0)
                mlp_down(HB - 1)

            body(0, True)
            with pe.Fori(1, NT - 1) as t:
                body(t, True)
            body(NT - 1, False)


_INS = ["x", "qkv_w", "qkv_b", "out_w", "out_b", "norm1_w", "norm2_w", "mlp_w1", "mlp_b1", "mlp_w2", "mlp_b2"]
_FFN_INS = ["fast_b", "w_fc", "w_proj", "u", "v", "gate"]


def kernel(**inputs):
    import concourse.bacc as bacc
    from concourse.bass_utils import run_bass_kernel_spmd

    nc = bacc.Bacc("TRN2", target_bir_lowering=False, num_devices=1, dynamic_dma_scratch_size=1024)
    arrays, args = {}, []
    for name in ["L0_attn_" + n for n in _INS] + ["L0_ffn_" + n for n in _FFN_INS]:
        a = np.ascontiguousarray(inputs[name])
        if a.ndim == 0:
            a = a.reshape(1, 1)
        arrays[name] = a
        args.append(nc.dram_tensor(name, a.shape, mybir.dt.from_np(a.dtype), kind="ExternalInput").ap())
    for name, a in zip(("consts", "trig"), constants()):
        arrays[name] = a
        args.append(nc.dram_tensor(name, a.shape, F32, kind="ExternalInput").ap())
    args.append(nc.dram_tensor("out", (B, L, E), F32, kind="ExternalOutput").ap())
    program(nc, *args)
    r = run_bass_kernel_spmd(nc, [arrays], core_ids=[0])
    return r.results[0]["out"]
```
